# Optimizing a Trainium2 kernel written in Bass

```python
import numpy as np
import jax
import jax.numpy as jnp

def _softmax(x, axis=-1):
    return jax.nn.softmax(x, axis=axis)

def _gelu(x):
    return jax.nn.gelu(x, approximate=True)

def _silu(x):
    return jax.nn.silu(x)

def _sigmoid(x):
    return jax.nn.sigmoid(x)

def _layernorm(x, axis=-1, eps=1e-05):
    m = jnp.mean(x, axis=axis, keepdims=True)
    v = jnp.var(x, axis=axis, keepdims=True)
    return (x - m) / jnp.sqrt(v + eps)

def _scatter_add(tgt, idx, src, axis=0):
    return tgt.at[idx].add(src)

def _segment_sum(src, seg, n):
    return jax.ops.segment_sum(src, seg, n)
kernel_name = 'mk_decoder_postln_d1_seqx_r4_14c534'

def setup_inputs(seed: int=0):
    np.random.seed(seed)
    _w = jnp.asarray

    def _rec_inputs():
        import jax
        import jax.numpy as jnp
        _rk = jax.random.key(seed)
        x = 7.22e-05 + 1 * jax.random.normal(jax.random.fold_in(_rk, 1), (4, 512, 256), jnp.float32)
        _lenS = 512 - jax.random.randint(jax.random.fold_in(_rk, 7), (4,), 0, max(1, 512 // 4) + 1, jnp.int32)
        _lenS2 = 512 - jax.random.randint(jax.random.fold_in(_rk, 8), (4,), 0, max(1, 512 // 4) + 1, jnp.int32)
        _ctx_1024P = jax.random.normal(jax.random.fold_in(_rk, 11), (4, 16, 256), jnp.float32)
        _ctx_1024c = jax.random.dirichlet(jax.random.fold_in(_rk, 511), 0.3 * jnp.ones((16,), jnp.float32), (4, 512))
        _ctx_1024t = jnp.einsum('bsk,bkd->bsd', _ctx_1024c, _ctx_1024P)
        _ctx_1024t = _ctx_1024t * jax.lax.rsqrt(jnp.mean(jnp.square(_ctx_1024t)) + 1e-12) * 0.953939
        ctx_1024 = 4.13588e-05 + 0.999923 * (_ctx_1024t + 0.3 * jax.random.normal(jax.random.fold_in(_rk, 611), (4, 512, 256), jnp.float32))
        return (x, ctx_1024)
    x, ctx_1024 = _rec_inputs()

    def _L0_attn_setup():
        import jax, jax.numpy as jnp
        from jax import lax
        import numpy as np
        D = 256
        H = 16
        DK = D // 2 // H
        DV = D // H
        GATE_NORM = 16.0
        SCALE = DK ** (-0.5)
        EPS = 1e-05

        def _split_heads(x, dh):
            B, L, _ = x.shape
            return x.reshape(B, L, H, dh).transpose(0, 2, 1, 3)

        def _gla_scan(q, k, v, log_gate):
            B = q.shape[0]
            qt = jnp.moveaxis(q, 2, 0)
            kt = jnp.moveaxis(k, 2, 0)
            vt = jnp.moveaxis(v, 2, 0)
            gt = jnp.exp(jnp.moveaxis(log_gate, 2, 0))

            def step(state, inp):
                qq, kk, vv, gg = inp
                state = state * gg[..., None] + kk[..., :, None] * vv[..., None, :]
                out = jnp.einsum('bhd,bhde->bhe', qq, state)
                return (state, out)
            init = jnp.zeros((B, H, DK, DV), dtype=q.dtype)
            _, outs = lax.scan(step, init, (qt, kt, vt, gt))
            return jnp.moveaxis(outs, 0, 2)
        key = jax.random.key(seed)
        ks = jax.random.split(key, 10)
        s = 0.02
        return {'inputs': jax.random.normal(ks[0], (4, 1024, D), dtype=jnp.float32), 'Wq': jax.random.normal(ks[1], (D, D // 2), dtype=jnp.float32) * s, 'Wk': jax.random.normal(ks[2], (D, D // 2), dtype=jnp.float32) * s, 'Wg1': jax.random.normal(ks[3], (D, 16), dtype=jnp.float32) * s, 'Wg2': jax.random.normal(ks[4], (16, D // 2), dtype=jnp.float32) * s, 'Wv': jax.random.normal(ks[5], (D, D), dtype=jnp.float32) * s, 'Wg': jax.random.normal(ks[6], (D, D), dtype=jnp.float32) * s, 'bg': jax.random.normal(ks[7], (D,), dtype=jnp.float32) * s, 'Wo': jax.random.normal(ks[8], (D, D), dtype=jnp.float32) * s}
    _L0_attn_all = _L0_attn_setup()
    _L0_attn_in = {k: v for k, v in _L0_attn_all.items() if k in ('Wq', 'Wk', 'Wg1', 'Wg2', 'Wv', 'Wg', 'bg', 'Wo')}
    del _L0_attn_all

    def _L0_xattn_setup():
        import jax, jax.numpy as jnp
        import numpy as np
        EMBED = 256
        HEADS = 16
        HEAD_DIM = EMBED // HEADS
        key = jax.random.key(seed)
        ks = jax.random.split(key, 7)
        B, Sd, Se = (4, 512, 512)
        dec = jax.random.normal(ks[0], (B, Sd, EMBED), dtype=jnp.float32)
        enc = jax.random.normal(ks[1], (B, Se, EMBED), dtype=jnp.float32)
        scale = 1.0 / np.sqrt(EMBED)
        W_q = jax.random.normal(ks[2], (EMBED, EMBED), dtype=jnp.float32) * scale
        W_k = jax.random.normal(ks[3], (EMBED, EMBED), dtype=jnp.float32) * scale
        W_v = jax.random.normal(ks[4], (EMBED, EMBED), dtype=jnp.float32) * scale
        W_o = jax.random.normal(ks[5], (EMBED, EMBED), dtype=jnp.float32) * scale
        b_o = jax.random.normal(ks[6], (EMBED,), dtype=jnp.float32) * 0.01
        return {'decoder_input': dec, 'encoder_output': enc, 'W_q': W_q, 'W_k': W_k, 'W_v': W_v, 'W_o': W_o, 'b_o': b_o}
    _L0_xattn_all = _L0_xattn_setup()
    _L0_xattn_in = {k: v for k, v in _L0_xattn_all.items() if k in ('W_q', 'W_k', 'W_v', 'W_o', 'b_o')}
    del _L0_xattn_all

    def _L0_ffn_setup():
        import jax, jax.numpy as jnp
        import numpy as np
        DIM = 256

        def _reference_tuple_inner(x, W_r, W_k, W_v, mu_r, mu_k):
            B, T, C = x.shape
            x_prev = jnp.concatenate([jnp.zeros((B, 1, C), x.dtype), x[:, :-1, :]], axis=1)
            xr = mu_r * x + (1.0 - mu_r) * x_prev
            xk = mu_k * x + (1.0 - mu_k) * x_prev
            r = jax.nn.sigmoid(jnp.einsum('btc,dc->btd', xr, W_r))
            k = jnp.einsum('btc,dc->btd', xk, W_k)
            k_act = jnp.square(jax.nn.relu(k))
            out = r * jnp.einsum('btc,dc->btd', k_act, W_v)
            new_state = x[:, -1, :]
            return (out, new_state)
        key = jax.random.key(seed)
        ks = jax.random.split(key, 6)
        B, T, C = (8, 512, DIM)
        x = jax.random.normal(ks[0], (B, T, C), dtype=jnp.float32)
        s = 1.0 / np.sqrt(C)
        W_r = jax.random.uniform(ks[1], (C, C), jnp.float32, -s, s)
        W_k = jax.random.uniform(ks[2], (C, C), jnp.float32, -s, s)
        W_v = jax.random.uniform(ks[3], (C, C), jnp.float32, -s, s)
        mu_r = jax.random.uniform(ks[4], (C,), jnp.float32)
        mu_k = jax.random.uniform(ks[5], (C,), jnp.float32)
        return {'x': x, 'W_r': W_r, 'W_k': W_k, 'W_v': W_v, 'mu_r': mu_r, 'mu_k': mu_k}
    _L0_ffn_all = _L0_ffn_setup()
    _L0_ffn_in = {k: v for k, v in _L0_ffn_all.items() if k in ('W_r', 'W_k', 'W_v', 'mu_r', 'mu_k')}
    del _L0_ffn_all
    return {'x': x, 'ctx_1024': ctx_1024, 'L0_attn_Wq': _L0_attn_in['Wq'], 'L0_attn_Wk': _L0_attn_in['Wk'], 'L0_attn_Wg1': _L0_attn_in['Wg1'], 'L0_attn_Wg2': _L0_attn_in['Wg2'], 'L0_attn_Wv': _L0_attn_in['Wv'], 'L0_attn_Wg': _L0_attn_in['Wg'], 'L0_attn_bg': _L0_attn_in['bg'], 'L0_attn_Wo': _L0_attn_in['Wo'], 'L0_xattn_W_q': _L0_xattn_in['W_q'], 'L0_xattn_W_k': _L0_xattn_in['W_k'], 'L0_xattn_W_v': _L0_xattn_in['W_v'], 'L0_xattn_W_o': _L0_xattn_in['W_o'], 'L0_xattn_b_o': _L0_xattn_in['b_o'], 'L0_ffn_W_r': _L0_ffn_in['W_r'], 'L0_ffn_W_k': _L0_ffn_in['W_k'], 'L0_ffn_W_v': _L0_ffn_in['W_v'], 'L0_ffn_mu_r': _L0_ffn_in['mu_r'], 'L0_ffn_mu_k': _L0_ffn_in['mu_k']}

def reference(x, ctx_1024, L0_attn_Wq, L0_attn_Wk, L0_attn_Wg1, L0_attn_Wg2, L0_attn_Wv, L0_attn_Wg, L0_attn_bg, L0_attn_Wo, L0_xattn_W_q, L0_xattn_W_k, L0_xattn_W_v, L0_xattn_W_o, L0_xattn_b_o, L0_ffn_W_r, L0_ffn_W_k, L0_ffn_W_v, L0_ffn_mu_r, L0_ffn_mu_k):
    import jax
    import jax.numpy as jnp

    def _L0_attn_ref(inputs, Wq, Wk, Wg1, Wg2, Wv, Wg, bg, Wo):
        import jax, jax.numpy as jnp
        from jax import lax
        import numpy as np
        D = 256
        H = 16
        DK = D // 2 // H
        DV = D // H
        GATE_NORM = 16.0
        SCALE = DK ** (-0.5)
        EPS = 1e-05

        def _split_heads(x, dh):
            B, L, _ = x.shape
            return x.reshape(B, L, H, dh).transpose(0, 2, 1, 3)

        def _gla_scan(q, k, v, log_gate):
            B = q.shape[0]
            qt = jnp.moveaxis(q, 2, 0)
            kt = jnp.moveaxis(k, 2, 0)
            vt = jnp.moveaxis(v, 2, 0)
            gt = jnp.exp(jnp.moveaxis(log_gate, 2, 0))

            def step(state, inp):
                qq, kk, vv, gg = inp
                state = state * gg[..., None] + kk[..., :, None] * vv[..., None, :]
                out = jnp.einsum('bhd,bhde->bhe', qq, state)
                return (state, out)
            init = jnp.zeros((B, H, DK, DV), dtype=q.dtype)
            _, outs = lax.scan(step, init, (qt, kt, vt, gt))
            return jnp.moveaxis(outs, 0, 2)
        B, L, _ = inputs.shape
        q = _split_heads(inputs @ Wq, DK)
        k = _split_heads(inputs @ Wk * SCALE, DK)
        kg = _split_heads(inputs @ Wg1 @ Wg2, DK)
        v = _split_heads(inputs @ Wv, DV)
        gate = jax.nn.silu(inputs @ Wg + bg)
        log_gate = jax.nn.log_sigmoid(kg) / GATE_NORM
        o = _gla_scan(q, k, v, log_gate)
        mu = jnp.mean(o, axis=-1, keepdims=True)
        var = jnp.var(o, axis=-1, keepdims=True)
        o = (o - mu) * lax.rsqrt(var + EPS)
        o = o.transpose(0, 2, 1, 3).reshape(B, L, D)
        return gate * o @ Wo

    def _L0_xattn_ref(decoder_input, encoder_output, W_q, W_k, W_v, W_o, b_o):
        import jax, jax.numpy as jnp
        import numpy as np
        EMBED = 256
        HEADS = 16
        HEAD_DIM = EMBED // HEADS
        B, Sd, E = decoder_input.shape
        Se = encoder_output.shape[1]
        Q = (decoder_input @ W_q).reshape(B, Sd, HEADS, HEAD_DIM)
        K = (encoder_output @ W_k).reshape(B, Se, HEADS, HEAD_DIM)
        V = (encoder_output @ W_v).reshape(B, Se, HEADS, HEAD_DIM)
        scores = jnp.einsum('bqhd,bkhd->bhqk', Q, K) / jnp.sqrt(jnp.float32(HEAD_DIM))
        attn = jax.nn.softmax(scores, axis=-1)
        out = jnp.einsum('bhqk,bkhd->bqhd', attn, V).reshape(B, Sd, E)
        return out @ W_o + b_o

    def _L0_ffn_ref(x, W_r, W_k, W_v, mu_r, mu_k):
        import jax, jax.numpy as jnp
        import numpy as np
        DIM = 256

        def _reference_tuple_inner(x, W_r, W_k, W_v, mu_r, mu_k):
            B, T, C = x.shape
            x_prev = jnp.concatenate([jnp.zeros((B, 1, C), x.dtype), x[:, :-1, :]], axis=1)
            xr = mu_r * x + (1.0 - mu_r) * x_prev
            xk = mu_k * x + (1.0 - mu_k) * x_prev
            r = jax.nn.sigmoid(jnp.einsum('btc,dc->btd', xr, W_r))
            k = jnp.einsum('btc,dc->btd', xk, W_k)
            k_act = jnp.square(jax.nn.relu(k))
            out = r * jnp.einsum('btc,dc->btd', k_act, W_v)
            new_state = x[:, -1, :]
            return (out, new_state)
        return _reference_tuple_inner(x, W_r, W_k, W_v, mu_r, mu_k)[0]
    x = _layernorm(x + _L0_attn_ref(x, L0_attn_Wq, L0_attn_Wk, L0_attn_Wg1, L0_attn_Wg2, L0_attn_Wv, L0_attn_Wg, L0_attn_bg, L0_attn_Wo), axis=-1)
    x = _layernorm(x + _L0_xattn_ref(x, ctx_1024, L0_xattn_W_q, L0_xattn_W_k, L0_xattn_W_v, L0_xattn_W_o, L0_xattn_b_o), axis=-1)
    x = _layernorm(x + _L0_ffn_ref(x, L0_ffn_W_r, L0_ffn_W_k, L0_ffn_W_v, L0_ffn_mu_r, L0_ffn_mu_k), axis=-1)
    return x

_drawn_inputs = setup_inputs


def setup_inputs(seed=0):
    import zlib

    import numpy as np

    out = dict(_drawn_inputs(seed))
    spreads = {}
    factors = {'L0_attn_Wg1': 59.397,
     'L0_attn_Wg2': 56.03,
     'L0_attn_bg': 8.0,
     'L0_xattn_b_o': 6.118,
     'L0_ffn_W_r': 2.796,
     'L0_ffn_mu_r': 6.584}
    for name, (base, spread) in spreads.items():
        noise = np.random.default_rng([zlib.crc32(name.encode()), seed]).standard_normal(out[name].shape)
        drawn = base * np.exp(spread * noise) if base else spread * noise
        out[name] = jnp.asarray(drawn.astype(out[name].dtype))
    for name, factor in factors.items():
        out[name] = (out[name] * factor).astype(out[name].dtype)
    return out
```

```python
from contextlib import ExitStack

import concourse.bass as bass
from concourse import mybir

ALU = mybir.AluOpType
ACT = mybir.ActivationFunctionType
F32 = mybir.dt.float32
BF16 = mybir.dt.bfloat16
AX = mybir.AxisListType

P = 128
B, S, D = 4, 512, 256
H = 16
DK, DV = 8, 16
HD = 16
ND = D // P
NT = S // P
NG = H // 4
EPS = 1e-5
LAG = 6
SLOTS_K = [0, 0, 1, 1, 0, 2]
SLOTS_Q = [0, 1, 0, 1, 2, 0]
NS = 16 * len(SLOTS_K)
NR = NS + 3

A_USES = ([("q", 0), ("k", 1), ("kg1", 2), ("v0", 0), ("v1", 1), ("kg", 2), ("z0", 0), ("z1", 1)]
          + [(f"vb{e}", 2) for e in range(DV)] + [("o0", 0), ("o1", 1), ("mean", 2), ("var", 2),
             ("y0", 0), ("y1", 1), ("t0", 2), ("t1", 0)])
B_USES = [("k0", 3), ("k1", 4), ("v0", 5), ("v1", 6), ("q0", 3), ("q1", 4)]
for _h in range(H):
    B_USES += [(f"m{_h}.{i}", 3 + i % 2) for i in range(NT)]
    if _h in (LAG - 2, LAG + 2, LAG + 6, H - 1):
        B_USES += [(f"mr{(_h - LAG + 2) // 4 if _h < H - 1 else 3}", 3)]
for _h in range(H):
    B_USES += [(f"s{_h}.{i}", 5 + i % 2) for i in range(NT)]
B_USES += [(f"pv{g}", 7) for g in range(NG)]
B_USES += [("y0", 3), ("y1", 4), ("t0", 5), ("t1", 6), ("r0", 3), ("r1", 4),
           ("f0", 5), ("f1", 6), ("w0", 3), ("w1", 4)]


def numbered(uses):
    count, out = {}, {}
    for name, bank in uses:
        count[bank] = count.get(bank, 0) + 1
        out[name] = (bank, count[bank])
    return out, count


A_AT, A_PER = numbered(A_USES)
B_AT, B_PER = numbered(B_USES)
A_FULL, A_FPER = numbered([u for u in A_USES if u[0] not in ("o0", "o1")])


FIRST = 1


def count(per, b, n):
    return b * per + (n + FIRST)


def held(eng, value):
    return value if isinstance(value, int) else eng.snap(value)


def build(nc, t):
    ctx = ExitStack()
    with ctx:
        def sb(name, shape, dt=F32):
            return ctx.enter_context(nc.sbuf_tensor(name, shape, dt))

        counting = []

        def sem(name):
            counting.append(ctx.enter_context(nc.semaphore(name)))
            return counting[-1]

        bank = [ctx.enter_context(nc.psum_tensor(f"bank{i}", [P, 512], F32)) for i in range(8)]
        full = [sem(f"bank{i}_full") for i in range(8)]
        free = [sem(f"bank{i}_free") for i in range(8)]

        wq = sb("wq", [P, ND, P])
        wk = sb("wk", [P, ND, P])
        wg1 = sb("wg1", [P, ND, 16])
        wg2 = sb("wg2", [16, P])
        wv = sb("wv", [P, ND, D])
        wg = sb("wg", [P, ND, D])
        bg = sb("bg", [P, ND])
        wo = sb("wo", [P, ND, D])
        xwq = sb("xwq", [P, ND, D])
        xwk = sb("xwk", [P, ND, D])
        xwv = sb("xwv", [P, ND, D])
        xwo = sb("xwo", [P, NG, D])
        xbo = sb("xbo", [P, D])
        fwr = sb("fwr", [P, ND, D])
        fwk = sb("fwk", [P, ND, D])
        fwv = sb("fwv", [P, ND, D])
        mur = sb("mur", [P, ND])
        muk = sb("muk", [P, ND])
        omr = sb("omr", [P, ND])
        omk = sb("omk", [P, ND])
        hsel = sb("hsel", [P, 2, 32])
        vsel = sb("vsel", [3 * H, P], BF16)
        mavg = sb("mavg", [P, P])
        ident = sb("ident", [P, P])
        identb = sb("identb", [P, P], BF16)
        vsel32 = sb("vsel32", [3 * H, P])
        eps = sb("eps", [P, 1])
        one = sb("one", [P, 1])
        mhalf = sb("mhalf", [P, NT])
        eps4 = sb("eps4", [P, NT])
        zero = sb("zero", [P, 16])
        xT = sb("xT", [P, ND, S])
        xtok = sb("xtok", [P, NT, D])
        qT = sb("qT", [P, S])
        kT = sb("kT", [P, S])
        kg1 = sb("kg1", [16, S])
        vT = sb("vT", [P, ND, S])
        vp = sb("vp", [P, 3, ND, S], BF16)
        VB = sb("VB", [3 * H, DV, S], BF16)
        kz = sb("kz", [P, 3, S])
        ab = sb("ab", [P, 3, S])
        U = sb("U", [P, 2, S])
        St = sb("St", [P, 2, S])
        Pq = sb("Pq", [P, 2, S])
        oS = sb("oS", [P, ND, S])
        sq = U
        rsd = ab[:, 1, :]
        x1 = sb("x1", [P, NT, D])
        x1b = sb("x1b", [P, NT, D])
        x1T = sb("x1T", [P, ND, S])
        cT = sb("cT", [P, ND, S])
        KT = sb("KT", [P, ND, S])
        kp = sb("kp", [P, 3, ND, S], BF16)
        QT, qp = KT, kp
        KS = sb("KS", [NR, H, S], BF16)
        QS = sb("QS", [NR, H, S], BF16)
        Vs = sb("Vs", [P, NT, H, 32])
        MX = sb("MX", [P, H * NT])
        MR = sb("MR", [P, 2, 16])
        MP = sb("MP", [P, 8, 16], BF16)
        mrow = sb("mrow", [48, P], BF16)
        PT = sb("PT", [P, 2, NT, S])
        den = sb("den", [P, S])
        spare = sb("spare", [P, 8])
        OT = sb("OT", [P, NG, S])
        x2 = sb("x2", [P, NT, D])
        x2T = sb("x2T", [P, ND, S + 1])
        xr, xk = PT[:, 0, 0:2, :], PT[:, 0, 2:4, :]
        ka, kaT = PT[:, 1, 0:2, :], PT[:, 1, 2:4, :]
        rl = OT[:, 0:2, :].rearrange("p a (t n) -> p (a t) n", n=D)
        ra = OT[:, 2:4, :].rearrange("p a (t n) -> p (a t) n", n=D)
        y3 = rl
        st = [sb(f"st{n}", [P, NT, 6]) for n in range(3)]
        mv = [sb(f"mv{n}", [P, NT, 2]) for n in range(3)]
        rs = [sb(f"rs{n}", [P, NT]) for n in range(3)]

        w_in = ctx.enter_context(nc.semaphore("w_in"))
        cst = ctx.enter_context(nc.semaphore("cst"))
        xT_in = sem("xT_in"); xt_in = sem("xt_in"); cT_in = sem("cT_in")
        v_hi = sem("v_hi"); v_r1 = sem("v_r1"); v_mid = sem("v_mid"); v_lo = sem("v_lo")
        v_out = sem("v_out"); v_in = sem("v_in")
        kz_abs = sem("kz_abs"); kz_exp = sem("kz_exp"); kz_ln = sem("kz_ln")
        kz_ls = sem("kz_ls"); kz_sig = sem("kz_sig"); gate_z = sem("gate_z")
        s_done = sem("s_done"); p_done = sem("p_done"); r_done = sem("r_done")
        o_sq = sem("o_sq"); o_rs = sem("o_rs")
        o_gate = sem("o_gate"); gated = sem("gated")
        st_done = [sem(f"st{n}_done") for n in range(3)]
        mv_done = [sem(f"mv{n}_done") for n in range(3)]
        ve_done = [sem(f"ve{n}_done") for n in range(3)]
        rs_done = [sem(f"rs{n}_done") for n in range(3)]
        x1_done = sem("x1_done"); x1b_done = sem("x1b_done")
        K_hi = sem("K_hi"); K_r1 = sem("K_r1"); K_mid = sem("K_mid"); K_lo = sem("K_lo")
        K_out = sem("K_out"); K_in = sem("K_in")
        Q_hi = sem("Q_hi"); Q_r1 = sem("Q_r1"); Q_mid = sem("Q_mid"); Q_lo = sem("Q_lo")
        Q_out = sem("Q_out"); Q_in = sem("Q_in")
        m_step = sem("m_step"); m_parts = sem("m_parts")
        m_in = sem("m_in"); pv_done = sem("pv_done")
        d_sh = sem("d_sh"); d_ln = sem("d_ln"); d_inv = sem("d_inv")

        x2_done = sem("x2_done"); mix_p = sem("mix_p"); mix_done = sem("mix_done")

        r_abs = sem("r_abs"); r_exp = sem("r_exp"); r_ln = sem("r_ln")
        r_ls = sem("r_ls"); r_sig = sem("r_sig"); ka2 = sem("ka2")
        f_mul = sem("f_mul"); x3_done = sem("x3_done"); o_out = sem("o_out")

        loads = [(wq, "wq"), (wk, "wk"), (wg1, "wg1"), (wg2, "wg2"), (wv, "wv"), (wg, "wg"), (bg, "bg"), (wo, "wo"),
                 (xwq, "xwq"), (xwk, "xwk"), (xwv, "xwv"), (xwo, "xwo"), (fwr, "fwr"), (fwk, "fwk"), (fwv, "fwv"),
                 (mur, "mur"), (muk, "muk"), (hsel, "hsel"), (vsel32, "vsel"), (mavg, "mavg"), (ident, "ident")]
        W_ALL = 16 * (len(loads) + 1)
        CST = 14
        out_v = t["out"].rearrange("b (t p) d -> b p t d", p=P)
        xtok_v = t["x"].rearrange("b (t p) d -> b p t d", p=P)


        def a_full(b, name):
            i, n = A_FULL[name]
            return full[i], count(A_FPER[i], b, n)

        def a_free(b, name):
            i, n = A_AT[name]
            return free[i], count(A_PER[i], b, n - 1)

        def a_read(b, name):
            i, n = A_AT[name]
            return free[i], count(A_PER[i], b, n)

        def a_done(b, name):
            i = A_AT[name][0]
            return full[i], count(A_FPER[i], b, 0)

        def b_full(b, name):
            i, n = B_AT[name]
            return full[i], count(B_PER[i], b, n)

        def b_free(b, name):
            i, n = B_AT[name]
            return free[i], count(B_PER[i], b, n - 1)

        def b_read(b, name):
            i, n = B_AT[name]
            return free[i], count(B_PER[i], b, n)

        def b_done(b, name):
            i = B_AT[name][0]
            return full[i], count(B_PER[i], b, 0)

        def a_full_sem(name):
            return full[A_AT[name][0]]

        def a_free_sem(name):
            return free[A_AT[name][0]]

        def b_full_sem(name):
            return full[B_AT[name][0]]

        def b_free_sem(name):
            return free[B_AT[name][0]]

        def abank(name):
            return bank[A_AT[name][0]]

        def bbank(name):
            return bank[B_AT[name][0]]

        def steps(eng, one_step):
            one_step(0, None)
            with eng.Fori(0, B - 1) as i:
                one_step(i + 1, i)
            one_step(None, B - 1)

        block = ctx.enter_context(nc.Block())

        @block.sync
        def _(sp):
            for dst, name in loads:
                full_ap = dst[tuple(slice(None) for _ in dst.shape)]
                sp.dma_start(full_ap, t[name]).then_inc(w_in, 16)
            sp.dma_start(xbo[:, :], t["xbo"][None, :].broadcast_to([P, D])).then_inc(w_in, 16)

            for s in counting:
                sp.sem_inc(s, FIRST)

            def one_step(a, b):
                if a is not None:
                    late = held(sp, a_done(a, "z1")[1])
                    sp.wait_ge(cst, CST)
                    sp.wait_ge(a_done(a, "z1")[0], late)
                    sp.dma_start(xT[:, :, :], t["xT"][a]).then_inc(xT_in, 16)
                    late = held(sp, count(NT, a, 0))
                    sp.wait_ge(cst, CST)
                    sp.wait_ge(x1_done, late)
                    sp.dma_start(xtok[:, :, :], xtok_v[a]).then_inc(xt_in, 16)
                if b is not None:
                    late = held(sp, b_done(b, "v1")[1])
                    sp.wait_ge(cst, CST)
                    sp.wait_ge(b_done(b, "v1")[0], late)
                    sp.dma_start(cT[:, :, :], t["cT"][b]).then_inc(cT_in, 16)
                if b is not None:
                    late = held(sp, count(1, b, 1))
                    sp.wait_ge(cst, CST)
                    sp.wait_ge(K_lo, late)
                    sp.dma_start(t["k_parts"][b].rearrange("s t p n -> p s t n"), kp[:, :, :, :]).then_inc(K_out, 16)
                if b is not None:
                    sp.wait_ge(K_out, count(16, b, 16))
                    sp.wait_ge(*b_done(b, f"s{H - 1}.{NT - 1}"))
                    late = held(sp, b_done(b, f"s{H - 1}.{NT - 2}")[1])
                    sp.wait_ge(cst, CST)
                    sp.wait_ge(b_done(b, f"s{H - 1}.{NT - 2}")[0], late)
                    for s, part in enumerate(SLOTS_K):
                        sp.dma_start(KS[HD * s:HD * s + HD, :, :],
                                     t["k_parts"][b, part].rearrange("t (h d) n -> d (t h) n", d=HD)).then_inc(K_in, 16)
                    late = held(sp, count(1, b, 1))
                    sp.wait_ge(cst, CST)
                    sp.wait_ge(Q_lo, late)
                    sp.dma_start(t["q_parts"][b].rearrange("s t p n -> p s t n"), qp[:, :, :, :]).then_inc(Q_out, 16)
                    late = held(sp, count(16, b, 16))
                    sp.wait_ge(cst, CST)
                    sp.wait_ge(Q_out, late)
                    for s, part in enumerate(SLOTS_Q):
                        sp.dma_start(QS[HD * s:HD * s + HD, :, :],
                                     t["q_parts"][b, part].rearrange("t (h d) n -> d (t h) n", d=HD)).then_inc(Q_in, 16)
                if a is not None:
                    late = held(sp, count(1, a, 1))
                    sp.wait_ge(cst, CST)
                    sp.wait_ge(v_lo, late)
                    sp.dma_start(t["v_parts"][a].rearrange("s t p n -> p s t n"), vp[:, :, :, :]).then_inc(v_out, 16)
                    sp.wait_ge(v_out, count(16, a, 16))
                    for s in range(3):
                        sp.dma_start(VB[H * s:H * s + H, :, :],
                                     t["v_parts"][a, s].rearrange("t (h e) n -> (t h) e n", e=DV)).then_inc(v_in, 16)
                if b is not None:
                    for g in range(NG):
                        late = held(sp, b_read(b, f"mr{g}")[1])
                        sp.wait_ge(cst, CST)
                        sp.wait_ge(b_read(b, f"mr{g}")[0], late)
                        for s in range(3):
                            sp.dma_start(QS[NS + s:NS + s + 1, 4 * g:4 * g + 4, :],
                                         mrow[16 * s:16 * s + 16, :]).then_inc(m_in, 16)
                    late = held(sp, count(NT, b, NT))
                    sp.wait_ge(cst, CST)
                    sp.wait_ge(x3_done, late)
                    sp.dma_start(out_v[b], y3[:, :, :]).then_inc(o_out, 16)

            steps(sp, one_step)
            sp.wait_ge(o_out, 16 * B + FIRST)
            sp.wait_ge(v_out, 16 * B + FIRST)
            sp.wait_ge(K_out, 16 * B + FIRST)
            sp.wait_ge(Q_out, 16 * B + FIRST)

        @block.tensor
        def _(pe):
            pe.wait_ge(w_in, W_ALL)
            pe.wait_ge(cst, CST)

            def project(out, w_of, x_of):
                for k in range(ND):
                    ins = pe.matmul(out, w_of(k), x_of(k), start=(k == 0), stop=(k == ND - 1))
                return ins

            def a_project(a):
                pe.wait_ge(xT_in, count(16, a, 16))
                x = lambda k: xT[:, k, :]
                pe.wait_ge(*a_free(a, "q"))
                project(abank("q")[:, :], lambda k: wq[:, k, :], x).then_inc(a_full_sem("q"), 1)
                pe.wait_ge(*a_free(a, "k"))
                project(abank("k")[:, :], lambda k: wk[:, k, :], x).then_inc(a_full_sem("k"), 1)
                pe.wait_ge(*a_free(a, "kg1"))
                project(abank("kg1")[0:16, :], lambda k: wg1[:, k, :], x).then_inc(a_full_sem("kg1"), 1)
                for m in range(ND):
                    pe.wait_ge(*a_free(a, f"v{m}"))
                    project(abank(f"v{m}")[:, :], lambda k: wv[:, k, m * P:(m + 1) * P], x).then_inc(a_full_sem(f"v{m}"), 1)
                pe.wait_ge(*a_read(a, "kg1"))
                pe.wait_ge(*a_free(a, "kg"))
                pe.matmul(abank("kg")[:, :], wg2[:, :], kg1[:, :], start=True, stop=True).then_inc(a_full_sem("kg"), 1)
                for m in range(ND):
                    pe.wait_ge(*a_free(a, f"z{m}"))
                    ins = project(abank(f"z{m}")[:, :], lambda k: wg[:, k, m * P:(m + 1) * P], x)
                    ins.then_inc(a_full_sem(f"z{m}"), 1)

            def state_step(a, e):
                if e == 0:
                    pe.wait_ge(v_in, count(48, a, 48))
                pe.wait_ge(*a_free(a, f"vb{e}"))
                pe.matmul(abank(f"vb{e}")[:, :], vsel[:, :], VB[:, e, :], start=True, stop=True).then_inc(a_full_sem(f"vb{e}"), 1)

            def reduce_step(a, e):
                g, j, i = e // 8, (e % 8) // 2, e % 2
                pe.wait_ge(p_done, count(DV, a, e + 1))
                if e % 8 == 0:
                    pe.wait_ge(*a_free(a, f"o{g}"))
                pe.matmul(abank(f"o{g}")[32 * j:32 * j + 32, :], hsel[:, i, :], Pq[:, e % 2, :],
                          start=(i == 0), stop=(i == 1)).then_inc(r_done, 1)

            def a_post(a):
                pe.wait_ge(*a_read(a, "o0"))
                pe.wait_ge(*a_read(a, "o1"))
                pe.wait_ge(*a_free(a, "mean"))
                project(abank("mean")[:, :], lambda k: mavg[:, :], lambda k: oS[:, k, :]).then_inc(a_full_sem("mean"), 1)
                pe.wait_ge(o_sq, count(1, a, 1))
                pe.wait_ge(*a_free(a, "var"))
                project(abank("var")[:, :], lambda k: mavg[:, :], lambda k: sq[:, k, :]).then_inc(a_full_sem("var"), 1)
                pe.wait_ge(gated, count(1, a, 1))
                for tt in range(NT):
                    n = f"y{tt // 2}"
                    if tt % 2 == 0:
                        pe.wait_ge(*a_free(a, n))
                    ins = project(abank(n)[:, (tt % 2) * D:(tt % 2 + 1) * D],
                                  lambda k: oS[:, k, tt * P:(tt + 1) * P], lambda k: wo[:, k, :])
                    if tt % 2:
                        ins.then_inc(a_full_sem(n), 1)
                pe.wait_ge(x1_done, count(NT, a, NT))
                for m in range(ND):
                    pe.wait_ge(*a_free(a, f"t{m}"))
                    for tt in range(NT):
                        ins = pe.transpose(abank(f"t{m}")[:, tt * P:(tt + 1) * P],
                                           x1[:, tt, m * P:(m + 1) * P], ident[:, :])
                    ins.then_inc(a_full_sem(f"t{m}"), 1)

            def b_context(b):
                pe.wait_ge(cT_in, count(16, b, 16))
                for m in range(ND):
                    pe.wait_ge(*b_free(b, f"k{m}"))
                    project(bbank(f"k{m}")[:, :], lambda k: xwk[:, k, m * P:(m + 1) * P],
                               lambda k: cT[:, k, :]).then_inc(b_full_sem(f"k{m}"), 1)
                for tt in range(NT):
                    n = f"v{tt // 2}"
                    if tt % 2 == 0:
                        pe.wait_ge(*b_free(b, n))
                    ins = project(bbank(n)[:, (tt % 2) * D:(tt % 2 + 1) * D],
                                  lambda k: cT[:, k, tt * P:(tt + 1) * P], lambda k: xwv[:, k, :])
                    if tt % 2:
                        ins.then_inc(b_full_sem(n), 1)

            def b_query(b):
                pe.wait_ge(*a_read(b, "t0"))
                pe.wait_ge(*a_read(b, "t1"))
                for m in range(ND):
                    pe.wait_ge(*b_free(b, f"q{m}"))
                    project(bbank(f"q{m}")[:, :], lambda k: xwq[:, k, m * P:(m + 1) * P],
                               lambda k: x1T[:, k, :]).then_inc(b_full_sem(f"q{m}"), 1)

            def max_tile(b, h, i):
                if h == 0 and i == 0:
                    pe.wait_ge(K_in, count(96, b, 96))
                    pe.wait_ge(Q_in, count(96, b, 96))
                n = f"m{h}.{i}"
                pe.wait_ge(*b_free(b, n))
                pe.matmul(bbank(n)[:, :], QS[0:NS, h, i * P:(i + 1) * P], KS[0:NS, h, :],
                             start=True, stop=True).then_inc(b_full_sem(n), 1)

            def max_rows(b, g):
                pe.wait_ge(m_parts, count(NG, b, g + 1))
                pe.wait_ge(*b_free(b, f"mr{g}"))
                pe.transpose(bbank(f"mr{g}")[:, 0:P // 2].bitcast(BF16),
                                MP[:, :, :].rearrange("p s n -> p (s n)"), identb[:, :]).then_inc(b_full_sem(f"mr{g}"), 1)

            def score_tile(b, h, i):
                if i == 0 and h % 4 == 0:
                    pe.wait_ge(m_in, count(48 * NG, b, 48 * (h // 4 + 1)))
                n = f"s{h}.{i}"
                pe.wait_ge(*b_free(b, n))
                ins = pe.matmul(bbank(n)[:, :], KS[0:NR, h, i * P:(i + 1) * P], QS[0:NR, h, :],
                                start=True, stop=True)
                ins.then_inc(b_full_sem(n), 1)

            def value_tile(b, h, i):
                g, j = h // 4, h % 4
                pe.wait_ge(*b_read(b, f"s{h}.{i}"))
                if h == 0 and i == 0:
                    pe.wait_ge(*b_read(b, "v0"))
                    pe.wait_ge(*b_read(b, "v1"))
                if j == 0 and i == 0:
                    pe.wait_ge(*b_free(b, f"pv{g}"))
                ins = pe.matmul(bbank(f"pv{g}")[32 * j:32 * j + 32, :], Vs[:, i, h, :], PT[:, h % 2, i, :],
                                start=(i == 0), stop=(i == NT - 1))
                if i == NT - 1:
                    ins.then_inc(pv_done, 1)

            def b_post(b):
                pe.wait_ge(*b_read(b, f"pv{NG - 1}"))
                for tt in range(NT):
                    n = f"y{tt // 2}"
                    if tt % 2 == 0:
                        pe.wait_ge(*b_free(b, n))
                    for g in range(NG):
                        ins = pe.matmul(bbank(n)[:, (tt % 2) * D:(tt % 2 + 1) * D],
                                        OT[:, g, tt * P:(tt + 1) * P], xwo[:, g, :],
                                        start=(g == 0), stop=(g == NG - 1))
                    if tt % 2:
                        ins.then_inc(b_full_sem(n), 1)
                pe.wait_ge(x2_done, count(NT, b, NT))
                for m in range(ND):
                    pe.wait_ge(*b_free(b, f"t{m}"))
                    for tt in range(NT):
                        ins = pe.transpose(bbank(f"t{m}")[:, tt * P:(tt + 1) * P],
                                           x2[:, tt, m * P:(m + 1) * P], ident[:, :])
                    ins.then_inc(b_full_sem(f"t{m}"), 1)

            def feed_forward(b):
                pe.wait_ge(mix_done, count(2, b, 1))
                for tt in range(NT):
                    n = f"r{tt // 2}"
                    if tt % 2 == 0:
                        pe.wait_ge(*b_free(b, n))
                    ins = project(bbank(n)[:, (tt % 2) * D:(tt % 2 + 1) * D],
                                  lambda k: xr[:, k, tt * P:(tt + 1) * P], lambda k: fwr[:, k, :])
                    if tt % 2:
                        ins.then_inc(b_full_sem(n), 1)
                pe.wait_ge(mix_done, count(2, b, 2))
                for m in range(ND):
                    pe.wait_ge(*b_free(b, f"f{m}"))
                    project(bbank(f"f{m}")[:, :], lambda k: fwk[:, k, m * P:(m + 1) * P],
                               lambda k: xk[:, k, :]).then_inc(b_full_sem(f"f{m}"), 1)
                pe.wait_ge(ka2, count(1, b, 1))
                for tt in range(NT):
                    n = f"w{tt // 2}"
                    if tt % 2 == 0:
                        pe.wait_ge(*b_free(b, n))
                    ins = project(bbank(n)[:, (tt % 2) * D:(tt % 2 + 1) * D],
                                  lambda k: kaT[:, k, tt * P:(tt + 1) * P], lambda k: fwv[:, k, :])
                    if tt % 2:
                        ins.then_inc(b_full_sem(n), 1)

            def one_step(a, b):
                if b is not None:
                    b_context(b)
                    b_query(b)
                if a is not None:
                    a_project(a)
                if b is not None:
                    for h in range(LAG):
                        for i in range(NT):
                            max_tile(b, h, i)
                        if h == LAG - 2:
                            max_rows(b, 0)
                for n in range(H + 1):
                    if a is not None and n < DV:
                        state_step(a, n)
                    if b is not None:
                        for i in range(NT):
                            if n + LAG < H:
                                max_tile(b, n + LAG, i)
                            if n < H:
                                score_tile(b, n, i)
                            if n >= 1:
                                value_tile(b, n - 1, i)
                        if n in (2, 6):
                            max_rows(b, n // 4 + 1)
                        if n == H - LAG - 1:
                            max_rows(b, 3)
                    if a is not None and n >= 1:
                        reduce_step(a, n - 1)
                if b is not None:
                    b_post(b)
                if a is not None:
                    a_post(a)
                if b is not None:
                    feed_forward(b)

            steps(pe, one_step)

        @block.scalar
        def _(act):
            act.preload_act_table_set("natural_log_exp_and_others")
            act.wait_ge(w_in, W_ALL)
            act.wait_ge(cst, CST)

            def a_pre(a):
                act.wait_ge(*a_full(a, "q"))
                act.wait_ge(p_done, count(DV, a, 0))
                act.activation(qT[:, :], abank("q")[:, :], ACT.Copy).then_inc(a_free_sem("q"), 1)
                act.wait_ge(*a_full(a, "k"))
                act.wait_ge(s_done, count(DV, a, 0))
                act.activation(kT[:, :], abank("k")[:, :], ACT.Copy, scale=float(DK) ** -0.5).then_inc(a_free_sem("k"), 1)
                act.wait_ge(*a_full(a, "kg1"))
                act.activation(kg1[:, :], abank("kg1")[0:16, :], ACT.Copy).then_inc(a_free_sem("kg1"), 1)
                for m in range(ND):
                    act.wait_ge(*a_full(a, f"v{m}"))
                    act.wait_ge(v_lo, count(1, a, 0))
                    act.activation(vT[:, m, :], abank(f"v{m}")[:, :], ACT.Copy).then_inc(a_free_sem(f"v{m}"), 1)
                act.wait_ge(*a_read(a, "v0"))
                act.wait_ge(*a_read(a, "v1"))
                act.wait_ge(v_out, count(16, a, 0))
                act.activation(vp[:, 0, :, :], vT[:, :, :], ACT.Copy).then_inc(v_hi, 1)
                act.wait_ge(*a_full(a, "kg"))
                act.wait_ge(s_done, count(DV, a, 0))
                act.wait_ge(o_gate, count(1, a, 0))
                act.activation(kz[:, 0, :], abank("kg")[:, :], ACT.Copy).then_inc(a_free_sem("kg"), 1)
                for m in range(ND):
                    act.wait_ge(*a_full(a, f"z{m}"))
                    act.activation(kz[:, 1 + m, :], abank(f"z{m}")[:, :], ACT.Identity, bias=bg[:, m:m + 1]).then_inc(a_free_sem(f"z{m}"), 1)
                act.wait_ge(v_r1, count(1, a, 1))
                act.activation(vp[:, 1, :, :], vT[:, :, :], ACT.Copy).then_inc(v_mid, 1)
                act.wait_ge(*a_read(a, "kg"))
                act.wait_ge(*a_read(a, "z0"))
                act.wait_ge(*a_read(a, "z1"))
                act.wait_ge(gated, count(1, a, 0))
                act.activation(ab[:, :, :], kz[:, :, :], ACT.Abs).then_inc(kz_abs, 1)
                act.wait_ge(kz_abs, count(1, a, 1))
                act.activation(ab[:, :, :], ab[:, :, :], ACT.Exp, scale=-1.0).then_inc(kz_exp, 1)
                act.wait_ge(kz_exp, count(1, a, 1))
                act.activation(ab[:, :, :], ab[:, :, :], ACT.Ln, bias=one[:, :]).then_inc(kz_ln, 1)
                act.wait_ge(kz_ls, count(1, a, 1))
                act.activation(ab[:, 0, :], ab[:, 0, :], ACT.Exp, scale=1.0 / 16.0).then_inc(kz_sig, 1)
                act.activation(ab[:, 1:3, :], ab[:, 1:3, :], ACT.Exp).then_inc(kz_sig, 1)

            def a_post(a, b):
                for g in range(ND):
                    act.wait_ge(r_done, count(DV, a, 8 * (g + 1)))
                    if g == 0:
                        act.wait_ge(*a_done(a, "y1"))
                    act.activation(oS[:, g, :], abank(f"o{g}")[:, :], ACT.Copy).then_inc(a_free_sem(f"o{g}"), 1)
                act.wait_ge(*a_full(a, "var"))
                act.wait_ge(gate_z, count(1, a, 1))
                act.activation(rsd, abank("var")[:, :], ACT.Ln, bias=eps[:, :]).then_inc(a_free_sem("var"), 1)
                act.wait_ge(*a_read(a, "var"))
                act.activation(rsd, rsd, ACT.Exp, scale=-0.5).then_inc(o_rs, 1)
                for m in range(ND):
                    act.wait_ge(*a_full(a, f"t{m}"))
                    if b is not None:
                        act.wait_ge(*b_full(b, "q1"))
                    act.activation(x1T[:, m, :], abank(f"t{m}")[:, :], ACT.Copy).then_inc(a_free_sem(f"t{m}"), 1)

            def b_context(b):
                for m in range(ND):
                    act.wait_ge(*b_full(b, f"k{m}"))
                    act.wait_ge(Q_lo, count(1, b, 0))
                    act.activation(KT[:, m, :], bbank(f"k{m}")[:, :], ACT.Copy).then_inc(b_free_sem(f"k{m}"), 1)
                act.wait_ge(*b_read(b, "k0"))
                act.wait_ge(*b_read(b, "k1"))
                act.wait_ge(Q_out, count(16, b, 0))
                act.activation(kp[:, 0, :, :], KT[:, :, :], ACT.Copy).then_inc(K_hi, 1)
                for m in range(ND):
                    act.wait_ge(*b_full(b, f"v{m}"))
                    act.wait_ge(pv_done, count(H, b, 0))
                    act.activation(Vs[:, 2 * m:2 * m + 2, :, 0:HD],
                                      bbank(f"v{m}")[:, :].rearrange("p (t h e) -> p t h e", t=2, e=HD), ACT.Copy).then_inc(b_free_sem(f"v{m}"), 1)
                act.wait_ge(K_r1, count(1, b, 1))
                act.activation(kp[:, 1, :, :], KT[:, :, :], ACT.Copy).then_inc(K_mid, 1)

            def b_query(b):
                for m in range(ND):
                    act.wait_ge(*b_full(b, f"q{m}"))
                    act.wait_ge(K_lo, count(1, b, 1))
                    act.activation(QT[:, m, :], bbank(f"q{m}")[:, :], ACT.Copy, scale=float(HD) ** -0.5).then_inc(b_free_sem(f"q{m}"), 1)
                act.wait_ge(*b_read(b, "q0"))
                act.wait_ge(*b_read(b, "q1"))
                act.wait_ge(K_out, count(16, b, 16))
                act.activation(qp[:, 0, :, :], QT[:, :, :], ACT.Copy).then_inc(Q_hi, 1)
                act.wait_ge(Q_r1, count(1, b, 1))
                act.activation(qp[:, 1, :, :], QT[:, :, :], ACT.Copy).then_inc(Q_mid, 1)

            def max_rows(b, g):
                act.wait_ge(*b_full(b, f"mr{g}"))
                act.wait_ge(m_in, count(48 * NG, b, 48 * g))
                act.activation(mrow[:, :], bbank(f"mr{g}")[0:48, 0:P // 2].bitcast(BF16), ACT.Copy).then_inc(b_free_sem(f"mr{g}"), 1)

            def exp_tile(b, h, i):
                n = f"s{h}.{i}"
                act.wait_ge(*b_full(b, n))
                if i == 0:
                    act.wait_ge(pv_done, count(H, b, max(h - 1, 0)))
                act.activation(PT[:, h % 2, i, :], bbank(n)[:, :], ACT.Exp).then_inc(b_free_sem(n), 1)

            def invert(b, g):
                act.wait_ge(d_sh, count(NG, b, g + 1))
                act.activation(den[:, :], den[:, :], ACT.Ln).then_inc(d_ln, 1)
                act.wait_ge(d_ln, count(NG, b, g + 1))
                act.activation(den[:, :], den[:, :], ACT.Exp, scale=-1.0).then_inc(d_inv, 1)

            def b_post(b):
                for m in range(ND):
                    act.wait_ge(*b_full(b, f"t{m}"))
                    act.wait_ge(mix_done, count(2, b, 0))
                    act.activation(x2T[:, m, 1:S + 1], bbank(f"t{m}")[:, :], ACT.Copy).then_inc(b_free_sem(f"t{m}"), 1)

            def feed_forward(b):
                for m in range(2):
                    act.wait_ge(*b_full(b, f"r{m}"))
                    act.wait_ge(r_ls, count(1, b, 0))
                    act.activation(rl[:, 2 * m:2 * m + 2, :],
                                      bbank(f"r{m}")[:, :].rearrange("p (t n) -> p t n", t=2), ACT.Copy).then_inc(b_free_sem(f"r{m}"), 1)
                for m in range(ND):
                    act.wait_ge(*b_full(b, f"f{m}"))
                    act.wait_ge(ka2, count(1, b, 0))
                    act.activation(ka[:, m, :], bbank(f"f{m}")[:, :], ACT.Relu).then_inc(b_free_sem(f"f{m}"), 1)
                act.wait_ge(*b_read(b, "r0"))
                act.wait_ge(*b_read(b, "r1"))
                act.activation(ra, rl, ACT.Abs).then_inc(r_abs, 1)
                act.wait_ge(r_abs, count(1, b, 1))
                act.activation(ra[:, :, :], ra[:, :, :], ACT.Exp, scale=-1.0).then_inc(r_exp, 1)
                act.wait_ge(r_exp, count(1, b, 1))
                act.activation(ra[:, :, :], ra[:, :, :], ACT.Ln, bias=one[:, :]).then_inc(r_ln, 1)
                act.wait_ge(r_ls, count(1, b, 1))
                act.activation(ra[:, :, :], ra[:, :, :], ACT.Exp).then_inc(r_sig, 1)

            def one_step(a, b):
                if b is not None:
                    b_context(b)
                    b_query(b)
                if a is not None:
                    a_pre(a)
                if b is not None:
                    max_rows(b, 0)
                    for n in range(H):
                        if n % 4 == 1 and n > 1:
                            invert(b, n // 4 - 1)
                        for i in range(NT):
                            exp_tile(b, n, i)
                        if n in (2, 6):
                            max_rows(b, n // 4 + 1)
                        if n == H - LAG - 1:
                            max_rows(b, 3)
                    invert(b, NG - 1)
                if b is not None:
                    b_post(b)
                if a is not None:
                    a_post(a, b)
                if b is not None:
                    feed_forward(b)

            steps(act, one_step)

        def norm(eng, n, src, dst, done, b):
            for tt in range(NT):
                ins = eng.bn_stats(st[n][:, tt, :], src[:, tt, :])
            ins.then_inc(st_done[n], 1)
            eng.wait_ge(st_done[n], count(1, b, 1))
            eng.tensor_copy(spare[:, 4 + n:5 + n], st[n][:, 0, 0:1])
            for tt in range(NT):
                ins = eng.bn_aggr(mv[n][:, tt, :], st[n][:, tt, :])
            ins.then_inc(mv_done[n], 1)
            eng.wait_ge(rs_done[n], count(1, b, 1))
            for tt in range(NT):
                eng.tensor_scalar(dst[:, tt, :], src[:, tt, :], mv[n][:, tt, 0:1], rs[n][:, tt:tt + 1],
                                  ALU.subtract, ALU.mult).then_inc(done, 1)

        def inverse_deviation(eng, n, b):
            eng.wait_ge(mv_done[n], count(1, b, 1))
            eng.tensor_tensor(rs[n][:, :], mv[n][:, :, 1], eps4[:, :], ALU.add).then_inc(ve_done[n], 1)
            eng.wait_ge(ve_done[n], count(1, b, 1))
            eng.tensor_tensor(rs[n][:, :], rs[n][:, :], mhalf[:, :], ALU.pow).then_inc(rs_done[n], 1)

        @block.vector
        def _(dve):
            dve.memset(eps[:, :], EPS).then_inc(cst, 1)
            dve.memset(eps4[:, :], EPS).then_inc(cst, 1)
            dve.memset(zero[:, :], 0.0).then_inc(cst, 1)
            dve.memset(MP[:, :, :], 0.0).then_inc(cst, 1)
            dve.memset(one[:, :], 1.0).then_inc(cst, 1)
            dve.memset(Vs[:, :, :, HD:HD + 1], 1.0).then_inc(cst, 1)
            dve.memset(Vs[:, :, :, HD + 1:32], 0.0).then_inc(cst, 1)
            dve.memset(KS[NS:NR, :, :], -1.0).then_inc(cst, 1)
            dve.memset(x2T[:, :, 0:1], 0.0).then_inc(cst, 1)
            dve.wait_ge(w_in, W_ALL)
            dve.tensor_copy(vsel[:, :], vsel32[:, :]).then_inc(cst, 1)
            dve.tensor_copy(identb[:, :], ident[:, :]).then_inc(cst, 1)
            dve.tensor_scalar(omr[:, :], mur[:, :], -1.0, 1.0, ALU.mult, ALU.add).then_inc(cst, 1)
            dve.tensor_scalar(omk[:, :], muk[:, :], -1.0, 1.0, ALU.mult, ALU.add).then_inc(cst, 1)
            dve.wait_ge(cst, CST)

            def a_pre(a):
                dve.wait_ge(kz_ln, count(1, a, 1))
                dve.scalar_tensor_tensor(ab[:, :, :], kz[:, :, :], 0.0, ab[:, :, :], ALU.min, ALU.subtract)\
                   .then_inc(kz_ls, 1)
                dve.wait_ge(kz_sig, count(2, a, 2))
                dve.tensor_tensor(kz[:, 1:3, :], kz[:, 1:3, :], ab[:, 1:3, :], ALU.mult).then_inc(gate_z, 1)

            def state_step(a, e):
                dve.wait_ge(*a_full(a, f"vb{e}"))
                if e == 0:
                    dve.wait_ge(*a_read(a, "k"))
                dve.tensor_tensor(U[:, e % 2, :], kT[:, :], abank(f"vb{e}")[:, :], ALU.mult).then_inc(a_free_sem(f"vb{e}"), 1)
                dve.wait_ge(*a_read(a, f"vb{e}"))
                dve.wait_ge(p_done, count(DV, a, max(e - 1, 0)))
                dve.tensor_tensor_scan(St[:, e % 2, :], ab[:, 0, :], U[:, e % 2, :], 0.0, ALU.mult, ALU.add)\
                   .then_inc(s_done, 1)

            def a_post(a):
                dve.wait_ge(*a_full(a, "mean"))
                mean = abank("mean")
                for g in range(ND):
                    ins = dve.tensor_tensor(oS[:, g, :], oS[:, g, :], mean[:, :], ALU.subtract)
                    if g == ND - 1:
                        ins.then_inc(a_free_sem("mean"), 1)
                for m in range(2):
                    dve.wait_ge(*a_full(a, f"y{m}"))
                    if m == 0:
                        dve.wait_ge(xt_in, count(16, a, 16))
                    dve.tensor_tensor(xtok[:, 2 * m:2 * m + 2, :],
                                         abank(f"y{m}")[:, :].rearrange("p (t n) -> p t n", t=2),
                                         xtok[:, 2 * m:2 * m + 2, :], ALU.add).then_inc(a_free_sem(f"y{m}"), 1)

            def a_norm(a):
                dve.wait_ge(*a_read(a, "y0"))
                dve.wait_ge(*a_read(a, "y1"))
                dve.wait_ge(x1b_done, count(1, a, 0))
                dve.wait_ge(*a_done(a, "t1"))
                norm(dve, 0, xtok, x1, x1_done, a)

            def max_tile(b, h, i):
                n = f"m{h}.{i}"
                dve.wait_ge(*b_full(b, n))
                dve.tensor_reduce(MX[:, NT * h + i:NT * h + i + 1], bbank(n)[:, :], AX.X, ALU.max).then_inc(b_free_sem(n), 1)

            def normalise(b, g):
                if g == 0:
                    dve.wait_ge(o_out, count(16, b, 0))
                    dve.wait_ge(*b_done(b, "y1"))
                dve.wait_ge(pv_done, count(H, b, 4 * (g + 1)))
                dve.tensor_copy(spare[:, g:g + 1], bbank(f"pv{g}")[:, 0:1])
                dve.stream_shuffle(den[:, :], bbank(f"pv{g}")[:, :], [HD] * 32).then_inc(d_sh, 1)

            def normalise_end(b, g):
                dve.wait_ge(d_inv, count(NG, b, g + 1))
                dve.tensor_tensor(OT[:, g, :], bbank(f"pv{g}")[:, :], den[:, :], ALU.mult).then_inc(b_free_sem(f"pv{g}"), 1)

            def residual(b, part, dst, res, m):
                return dve.tensor_tensor(dst[:, 2 * m:2 * m + 2, :],
                                         bbank(f"{part}{m}")[:, :].rearrange("p (t n) -> p t n", t=2),
                                         res[:, 2 * m:2 * m + 2, :], ALU.add)

            def b_post(b):
                for m in range(2):
                    dve.wait_ge(*b_full(b, f"y{m}"))
                    residual(b, "y", x1b, x1b, m).then_inc(b_free_sem(f"y{m}"), 1)
                dve.wait_ge(*b_read(b, "y0"))
                dve.wait_ge(*b_read(b, "y1"))
                dve.wait_ge(*b_done(b, "t1"))
                dve.wait_ge(x3_done, count(NT, b, 0))
                norm(dve, 1, x1b, x2, x2_done, b)

            def feed_forward(b):
                dve.wait_ge(*b_read(b, "t0"))
                dve.wait_ge(*b_read(b, "t1"))
                for which, (mu, dst) in enumerate(((mur, xr), (muk, xk))):
                    dve.wait_ge(mix_p, count(2, b, which + 1))
                    for m in range(ND):
                        ins = dve.scalar_tensor_tensor(dst[:, m, :], x2T[:, m, 1:S + 1], mu[:, m:m + 1], dst[:, m, :],
                                                       ALU.mult, ALU.add)
                    ins.then_inc(mix_done, 1)
                dve.wait_ge(r_ln, count(1, b, 1))
                dve.scalar_tensor_tensor(ra[:, :, :], rl[:, :, :], 0.0, ra[:, :, :], ALU.min, ALU.subtract)\
                   .then_inc(r_ls, 1)
                dve.wait_ge(r_sig, count(1, b, 1))
                for m in range(2):
                    dve.wait_ge(*b_full(b, f"w{m}"))
                    dve.tensor_tensor(ra[:, 2 * m:2 * m + 2, :],
                                         bbank(f"w{m}")[:, :].rearrange("p (t n) -> p t n", t=2),
                                         ra[:, 2 * m:2 * m + 2, :], ALU.mult).then_inc(b_free_sem(f"w{m}"), 1)
                dve.wait_ge(*b_read(b, "w0"))
                dve.wait_ge(*b_read(b, "w1"))
                dve.tensor_tensor(ra[:, :, :], ra[:, :, :], x2[:, :, :], ALU.add).then_inc(f_mul, 1)
                dve.wait_ge(f_mul, count(1, b, 1))
                norm(dve, 2, ra, y3, x3_done, b)

            def one_step(a, b):
                if a is not None:
                    a_pre(a)
                if b is not None:
                    for h in range(LAG):
                        for i in range(NT):
                            max_tile(b, h, i)
                for n in range(H + 1):
                    if a is not None and n < DV:
                        state_step(a, n)
                    if b is not None:
                        if n % 4 == 1 and n > 1:
                            normalise(b, n // 4 - 1)
                            normalise_end(b, n // 4 - 1)
                        if n + LAG < H:
                            for i in range(NT):
                                max_tile(b, n + LAG, i)
                if b is not None:
                    normalise(b, NG - 1)
                    normalise_end(b, NG - 1)
                if b is not None:
                    b_post(b)
                if a is not None:
                    a_post(a)
                    a_norm(a)
                if b is not None:
                    feed_forward(b)

            steps(dve, one_step)

        @block.gpsimd
        def _(pool):
            pool.memset(mhalf[:, :], -0.5).then_inc(cst, 1)
            pool.wait_ge(w_in, W_ALL)
            pool.wait_ge(cst, CST)

            def split(src, dst, hi, r1, mid, lo, per, b):
                pool.wait_ge(hi, count(1, b, 1))
                pool.tensor_tensor(src[:, :, :], src[:, :, :], dst[:, 0, :, :], ALU.subtract).then_inc(r1, 1)
                pool.wait_ge(mid, count(1, b, 1))
                pool.tensor_tensor(dst[:, 2, :, :], src[:, :, :], dst[:, 1, :, :], ALU.subtract).then_inc(lo, 1)

            def query_step(a, e):
                pool.wait_ge(s_done, count(DV, a, e + 1))
                if e == 0:
                    pool.wait_ge(*a_read(a, "q"))
                pool.wait_ge(r_done, count(DV, a, max(e - 1, 0)))
                pool.tensor_tensor(Pq[:, e % 2, :], qT[:, :], St[:, e % 2, :], ALU.mult).then_inc(p_done, 1)

            def max_parts(b, g):
                i, n = B_AT[f"m{4 * g + 3}.{NT - 2}"]
                pool.wait_ge(free[i], count(B_PER[i], b, n))
                if g:
                    pool.wait_ge(*b_full(b, f"mr{g - 1}"))
                else:
                    pool.wait_ge(*b_done(b, f"mr{NG - 1}"))
                pool.wait_ge(*b_read(b, f"m{4 * g + 3}.{NT - 1}"))
                m = MX[:, 16 * g:16 * g + 16]
                ops = [lambda: pool.tensor_tensor(MP[:, 0, :], m, zero[:, :], ALU.add),
                       lambda: pool.tensor_tensor(MR[:, 0, :], m, MP[:, 0, :], ALU.subtract),
                       lambda: pool.tensor_tensor(MP[:, 1, :], MR[:, 0, :], zero[:, :], ALU.add)]
                for k, op in enumerate(ops):
                    op().then_inc(m_step, 1)
                    pool.wait_ge(m_step, count(3 * NG, b, 3 * g + k + 1))
                pool.tensor_tensor(MP[:, 2, :], MR[:, 0, :], MP[:, 1, :], ALU.subtract).then_inc(m_parts, 1)

            def one_step(a, b):
                if b is not None:
                    split(KT, kp, K_hi, K_r1, K_mid, K_lo, 1, b)
                    split(QT, qp, Q_hi, Q_r1, Q_mid, Q_lo, 1, b)
                if a is not None:
                    split(vT, vp, v_hi, v_r1, v_mid, v_lo, 1, a)
                if b is not None:
                    max_parts(b, 0)
                for n in range(H + 1):
                    if a is not None and n < DV:
                        query_step(a, n)
                    if b is not None:
                        if n in (2, 6):
                            max_parts(b, n // 4 + 1)
                        if n == H - LAG - 1:
                            max_parts(b, 3)
                if b is not None:
                    inverse_deviation(pool, 1, b)
                if a is not None:
                    pool.wait_ge(*a_read(a, "mean"))
                    pool.wait_ge(s_done, count(DV, a, DV))
                    pool.tensor_tensor(sq[:, :, :], oS[:, :, :], oS[:, :, :], ALU.mult).then_inc(o_sq, 1)
                    pool.wait_ge(gate_z, count(1, a, 1))
                    pool.tensor_tensor(oS[:, :, :], oS[:, :, :], kz[:, 1:3, :], ALU.mult).then_inc(o_gate, 1)
                    pool.wait_ge(o_rs, count(1, a, 1))
                    pool.wait_ge(o_gate, count(1, a, 1))
                    pool.tensor_tensor(oS[:, :, :], oS[:, :, :], rsd.unsqueeze(1).broadcast_to([P, ND, S]),
                                       ALU.mult).then_inc(gated, 1)
                    inverse_deviation(pool, 0, a)
                    pool.wait_ge(x1_done, count(NT, a, NT))
                    if b is not None:
                        pool.wait_ge(x2_done, count(NT, b, NT))
                    pool.tensor_tensor(x1b[:, :, :], x1[:, :, :], xbo[:, :].unsqueeze(1).broadcast_to([P, NT, D]),
                                       ALU.add).then_inc(x1b_done, 1)
                if b is not None:
                    pool.wait_ge(*b_read(b, "t0"))
                    pool.wait_ge(*b_read(b, "t1"))
                    for which, (om, dst, last) in enumerate(((omr, xr, "r1"), (omk, xk, "f1"))):
                        pool.wait_ge(*b_done(b, last))
                        for m in range(ND):
                            ins = pool.tensor_tensor(dst[:, m, :], x2T[:, m, 0:S], om[:, m:m + 1].broadcast_to([P, S]), ALU.mult)
                        ins.then_inc(mix_p, 1)
                    pool.wait_ge(*b_read(b, "f0"))
                    pool.wait_ge(*b_read(b, "f1"))
                    pool.wait_ge(*b_done(b, "w1"))
                    pool.tensor_tensor(kaT[:, :, :], ka[:, :, :], ka[:, :, :], ALU.mult).then_inc(ka2, 1)
                    inverse_deviation(pool, 2, b)

            steps(pool, one_step)



def layouts(i):
    import numpy as np

    def rows(w):
        return np.ascontiguousarray(w.reshape(-1, P, w.shape[1]).transpose(1, 0, 2))

    def by_feature(x):
        return np.ascontiguousarray(x.transpose(0, 2, 1).reshape(B, ND, P, S).transpose(0, 2, 1, 3))

    eh = np.arange(D).reshape(H, DV).T.reshape(-1)
    xwo = np.zeros((NG, 4, 32, D), np.float32)
    xwo[:, :, :HD] = i["L0_xattn_W_o"].reshape(NG, 4, HD, D)
    hsel = np.zeros((P, 2, 32), np.float32)
    vsel = np.zeros((3 * H, P), np.float32)
    for r in range(P):
        for s in range(2):
            hsel[r, s, 16 * s + r // DK] = 1
        for s in range(3):
            vsel[H * s + r // DK, r] = 1
    r = np.arange(P)
    mavg = ((r[:, None] % H) == (r[None, :] % H)).astype(np.float32) / DV
    return {
        "x": i["x"], "xT": by_feature(i["x"]), "cT": by_feature(i["ctx_1024"]),
        "wq": rows(i["L0_attn_Wq"]), "wk": rows(i["L0_attn_Wk"]), "wg1": rows(i["L0_attn_Wg1"]),
        "wg2": i["L0_attn_Wg2"], "wv": rows(i["L0_attn_Wv"]),
        "wg": rows(i["L0_attn_Wg"][:, eh]), "bg": np.ascontiguousarray(i["L0_attn_bg"][eh].reshape(ND, P).T),
        "wo": rows(i["L0_attn_Wo"][eh]),
        "xwq": rows(i["L0_xattn_W_q"]), "xwk": rows(i["L0_xattn_W_k"]), "xwv": rows(i["L0_xattn_W_v"]),
        "xwo": np.ascontiguousarray(xwo.reshape(NG, P, D).transpose(1, 0, 2)), "xbo": i["L0_xattn_b_o"],
        "fwr": rows(i["L0_ffn_W_r"].T), "fwk": rows(i["L0_ffn_W_k"].T), "fwv": rows(i["L0_ffn_W_v"].T),
        "mur": np.ascontiguousarray(i["L0_ffn_mu_r"].reshape(ND, P).T),
        "muk": np.ascontiguousarray(i["L0_ffn_mu_k"].reshape(ND, P).T),
        "hsel": hsel, "vsel": vsel, "mavg": mavg,
        "ident": np.eye(P, dtype=np.float32),
    }


def kernel(**inputs):
    import numpy as np
    import concourse.bacc as bacc
    from concourse.bass_utils import run_bass_kernel_spmd

    nc = bacc.Bacc("TRN2", target_bir_lowering=False, num_devices=1)
    arrays, t = {}, {}
    for name, a in layouts({k: np.asarray(v) for k, v in inputs.items()}).items():
        arrays[f"in_{name}"] = np.ascontiguousarray(a)
        t[name] = nc.dram_tensor(f"in_{name}", a.shape, mybir.dt.from_np(a.dtype), kind="ExternalInput").ap()
    for name in ("v_parts", "k_parts", "q_parts"):
        t[name] = nc.dram_tensor(name, (B, 3, ND, P, S), BF16, kind="Internal").ap()
    t["out"] = nc.dram_tensor("out_0", (B, S, D), F32, kind="ExternalOutput").ap()
    build(nc, t)
    r = run_bass_kernel_spmd(nc, [arrays], core_ids=[0])
    return r.results[0]["out_0"]
```

```python
from contextlib import ExitStack

import concourse.bass as bass
from concourse import mybir

ALU = mybir.AluOpType
ACT = mybir.ActivationFunctionType
F32 = mybir.dt.float32
BF16 = mybir.dt.bfloat16
AX = mybir.AxisListType

P = 128
B, S, D = 4, 512, 256
H = 16
DK, DV = 8, 16
HD = 16
ND = D // P
NT = S // P
NG = H // 4
EPS = 1e-5
LAG = 5
SLOTS_K = [0, 0, 1, 1, 0, 2]
SLOTS_Q = [0, 1, 0, 1, 2, 0]
NS = 16 * len(SLOTS_K)
NR = NS + 3

STEPS = range(-2, B + 1)


def stages(s):
    return [x if 0 <= x < B else None for x in (s + 2, s + 1, s, s - 1)]


SIDE_USES = {
    (0, 0): ("V0", "b", 2), (0, 1): ("V1", "b", 0),
    (1, 0): ("gv0", "r", 1), (1, 1): ("gv1", "r", 2), (1, 2): ("mean", "o", 0), (1, 3): ("gg1", "r", 1),
    (2, 0): ("y0", "f", 2), (2, 1): ("y1", "f", 0), (2, 2): ("var", "o", 1), (2, 3): ("gg", "r", 2),
    (3, 0): ("gq", "r", 0), (3, 1): ("gk", "r", 1), (3, 2): ("K0", "o", 2), (3, 3): ("K1", "o", 0),
    (4, 0): ("t0", "f", 1), (4, 1): ("t1", "f", 2), (4, 2): ("gy0", "o", 0), (4, 3): ("gy1", "o", 1),
    (5, 0): ("gz0", "r", 2), (5, 1): ("gz1", "r", 0), (5, 2): ("r0", "f", 1), (5, 3): ("r1", "f", 2),
    (6, 0): ("gt0", "o", 0), (6, 1): ("gt1", "o", 1), (6, 2): ("f0", "f", 2), (6, 3): ("f1", "f", 0),
    (7, 0): ("Q0", "o", 1), (7, 1): ("Q1", "o", 2), (8, 1): ("w0", "f", 0), (8, 3): ("w1", "f", 0),
    (9, 1): ("o0", "r", 0), (13, 1): ("o1", "r", 1),
}
for _e in range(DV):
    SIDE_USES[8 + _e // 2, 2 * (_e % 2)] = (f"vb{_e}", "r", 2 if _e % 2 == 0 else 1 if _e < 11 else 0)


def number_uses():
    uses, signals, at = {}, {}, {}

    def use(name, batch, bank):
        if batch is None:
            return
        uses[bank] = uses.get(bank, 0) + 1
        if name not in ("o0", "o1"):
            signals[bank] = signals.get(bank, 0) + 1
        at[name, batch] = (bank, uses[bank], signals.get(bank, 0))

    for s in STEPS:
        stage = dict(zip("robf", stages(s)))
        for n in range(H):
            for i in range(NT):
                if (n, i) in SIDE_USES:
                    name, which, bank = SIDE_USES[n, i]
                    use(name, stage[which], bank)
                if n % 4 == 3 and i == 1:
                    use(f"mr{(n + 1) // 4 % NG}", stage["b" if n < H - 1 else "o"], 3)
                use(f"m{(n + LAG) % H}.{i}", stage["b" if n + LAG < H else "o"], 3 + i % 2)
                use(f"s{n}.{i}", stage["b"], 5 + i % 2)
                if n % 4 == 1 and i == 0:
                    use(f"pv{n // 4}", stage["b"], 7)
    return at


USES = number_uses()
BANK = {name: use[0] for (name, _), use in USES.items()}

FIRST = 1


def count(per, b, n):
    return b * per + (n + FIRST)


def build(nc, t):
    ctx = ExitStack()
    with ctx:
        def sb(name, shape, dt=F32):
            return ctx.enter_context(nc.sbuf_tensor(name, shape, dt))

        counting = []

        def sem(name):
            counting.append(ctx.enter_context(nc.semaphore(name)))
            return counting[-1]

        banks = [ctx.enter_context(nc.psum_tensor(f"bank{i}", [P, 512], F32)) for i in range(8)]
        full = [sem(f"bank{i}_full") for i in range(8)]
        free = [sem(f"bank{i}_free") for i in range(8)]

        wq = sb("wq", [P, ND, P])
        wk = sb("wk", [P, ND, P])
        wg1 = sb("wg1", [P, ND, 16])
        wg2 = sb("wg2", [16, P])
        wv = sb("wv", [P, ND, D])
        wg = sb("wg", [P, ND, D])
        bg = sb("bg", [P, ND])
        wo = sb("wo", [P, ND, D])
        xwq = sb("xwq", [P, ND, D])
        xwk = sb("xwk", [P, ND, D])
        xwv = sb("xwv", [P, ND, D])
        xwo = sb("xwo", [P, NG, D])
        xbo = sb("xbo", [P, D])
        fwr = sb("fwr", [P, ND, D])
        fwk = sb("fwk", [P, ND, D])
        fwv = sb("fwv", [P, ND, D])
        mur = sb("mur", [P, ND])
        muk = sb("muk", [P, ND])
        omr = sb("omr", [P, ND])
        omk = sb("omk", [P, ND])
        hsel = sb("hsel", [P, 2, 32])
        vsel = sb("vsel", [3 * H, P], BF16)
        mavg = sb("mavg", [P, P])
        ident = sb("ident", [P, P])
        identb = sb("identb", [P, P], BF16)
        vsel32 = sb("vsel32", [3 * H, P])
        eps = sb("eps", [P, 1])
        one = sb("one", [P, 1])
        mhalf = sb("mhalf", [P, NT])
        eps4 = sb("eps4", [P, NT])
        zero = sb("zero", [P, 16])
        xT = sb("xT", [P, ND, S])
        xtok = sb("xtok", [P, NT, D])
        qT = sb("qT", [P, S])
        kT = sb("kT", [P, S])
        kg1 = sb("kg1", [16, S])
        VB = sb("VB", [3 * H, DV, S], BF16)
        kz = sb("kz", [P, 3, S])
        ab = sb("ab", [P, 3, S])
        U = sb("U", [P, 2, S])
        St = sb("St", [P, 2, S])
        Pq = sb("Pq", [P, 2, S])
        oS = sb("oS", [P, ND, S])
        sq = U
        rsd = ab[:, 1, :]
        x1 = sb("x1", [P, NT, D])
        x1b = sb("x1b", [P, 2, NT, D])
        x1T = sb("x1T", [P, ND, S])
        full32 = sb("full32", [P, ND, S])
        parts = sb("parts", [P, 3, ND, S], BF16)
        cT = sb("cT", [P, ND, S])
        KS = sb("KS", [NR, H, S], BF16)
        QS = sb("QS", [NR, H, S], BF16)
        Vs = sb("Vs", [P, NT, H, 32])
        MX = sb("MX", [P, H * NT])
        MR = sb("MR", [P, 2, 16])
        MP = sb("MP", [P, 8, 16], BF16)
        mrow = sb("mrow", [48, P], BF16)
        PT = sb("PT", [P, 2, NT, S])
        den = sb("den", [P, S])
        OT = sb("OT", [P, NG, S])
        x2 = sb("x2", [P, NT, D])
        x2T = sb("x2T", [P, ND, S + 1])
        xr = sb("xr", [P, ND, S])
        xk = sb("xk", [P, ND, S])
        ka = sb("ka", [P, ND, S])
        rl = sb("rl", [P, NT, D])
        ra = xr[:, :, :].rearrange("p a (t n) -> p (a t) n", n=D)
        y3 = rl
        st = [sb(f"st{n}", [P, NT, 6]) for n in range(3)]
        mv = [sb(f"mv{n}", [P, NT, 2]) for n in range(3)]
        rs = [sb(f"rs{n}", [P, NT]) for n in range(3)]

        w_in = ctx.enter_context(nc.semaphore("w_in"))
        w2_in = ctx.enter_context(nc.semaphore("w2_in"))
        cst = ctx.enter_context(nc.semaphore("cst"))
        ks_set = ctx.enter_context(nc.semaphore("ks_set"))
        xT_in = sem("xT_in"); xt_in = sem("xt_in"); cT_in = sem("cT_in")
        v_hi = sem("v_hi"); v_r1 = sem("v_r1"); v_mid = sem("v_mid"); v_lo = sem("v_lo")
        v_out = sem("v_out"); v_in = sem("v_in")
        kz_abs = sem("kz_abs"); kz_exp = sem("kz_exp"); kz_ln = sem("kz_ln")
        kz_ls = sem("kz_ls"); kz_sig = sem("kz_sig"); gate_z = sem("gate_z")
        s_done = sem("s_done"); p_done = sem("p_done"); r_done = sem("r_done")
        o_sq = sem("o_sq"); o_rs = sem("o_rs"); o_gate = sem("o_gate"); gated = sem("gated")
        st_done = [sem(f"st{n}_done") for n in range(3)]
        mv_done = [sem(f"mv{n}_done") for n in range(3)]
        ve_done = [sem(f"ve{n}_done") for n in range(3)]
        rs_done = [sem(f"rs{n}_done") for n in range(3)]
        x1_done = sem("x1_done"); x1b_done = sem("x1b_done")
        K_hi = sem("K_hi"); K_r1 = sem("K_r1"); K_mid = sem("K_mid"); K_lo = sem("K_lo"); K_out = sem("K_out")
        Q_hi = sem("Q_hi"); Q_r1 = sem("Q_r1"); Q_mid = sem("Q_mid"); Q_lo = sem("Q_lo"); Q_out = sem("Q_out")
        K_in = [sem(f"K_in{g}") for g in range(NG)]
        Q_in = [sem(f"Q_in{g}") for g in range(NG)]
        m_step = sem("m_step"); m_parts = sem("m_parts"); m_in = sem("m_in")
        pv_done = sem("pv_done"); d_sh = sem("d_sh"); d_ln = sem("d_ln"); d_inv = sem("d_inv"); normal = sem("normal")
        x2_done = sem("x2_done"); mix_p = sem("mix_p"); mix_done = sem("mix_done")
        r_abs = sem("r_abs"); r_exp = sem("r_exp"); r_ln = sem("r_ln"); r_ls = sem("r_ls"); r_sig = sem("r_sig")
        ka2 = sem("ka2"); w_mul = sem("w_mul"); f_mul = sem("f_mul"); x3_done = sem("x3_done"); o_out = sem("o_out")

        loads = [(wv, "wv"), (wg1, "wg1"), (wg2, "wg2"), (vsel32, "vsel"), (wq, "wq"), (wk, "wk"), (wg, "wg"),
                 (bg, "bg"), (ident, "ident"), (mur, "mur"), (muk, "muk"), (hsel, "hsel"), (mavg, "mavg")]
        loads2 = [(xwk, "xwk"), (wo, "wo"), (xwq, "xwq"), (xwv, "xwv"), (xwo, "xwo"),
                  (fwr, "fwr"), (fwk, "fwk"), (fwv, "fwv")]
        W_ALL = 16 * len(loads)
        W2_ALL = 16 * (len(loads2) + 1)
        CST = 11
        out_v = t["out"].rearrange("b (t p) d -> b p t d", p=P)
        xtok_v = t["x"].rearrange("b (t p) d -> b p t d", p=P)


        def full_of(name, b):
            bank, _, signal = USES.get((name, b), (0, 0, 0))
            return full[bank], signal + FIRST

        def free_for(name, b):
            bank, use, _ = USES[name, b]
            return free[bank], use - 1 + FIRST

        def read(name, b):
            bank, use, _ = USES[name, b]
            return free[bank], use + FIRST

        def filled(name):
            return full[BANK[name]]

        def emptied(name):
            return free[BANK[name]]

        def bank(name):
            return banks[BANK[name]]

        def tokens(name):
            return bank(name)[:, :].rearrange("p (t n) -> p t n", t=2)

        block = ctx.enter_context(nc.Block())

        @block.sync
        def _(sp):
            sp.dma_start(xT[:, :, :], t["xT"][0]).then_inc(xT_in, 16)
            for dst, name in loads:
                sp.dma_start(dst[tuple(slice(None) for _ in dst.shape)], t[name]).then_inc(w_in, 16)
            for s in counting:
                sp.sem_inc(s, FIRST)
            sp.dma_start(cT[:, :, :], t["cT"][0]).then_inc(cT_in, 16)
            for dst, name in loads2:
                sp.dma_start(dst[tuple(slice(None) for _ in dst.shape)], t[name]).then_inc(w2_in, 16)
            sp.dma_start(xbo[:, :], t["xbo"][None, :].broadcast_to([P, D])).then_inc(w2_in, 16)
            sp.dma_start(xtok[:, :, :], xtok_v[0]).then_inc(xt_in, 16)

            def keys_in(b, g):
                sp.wait_ge(ks_set, 3)
                sp.wait_ge(K_out, count(16, b, 16))
                sp.wait_ge(*full_of(f"s{4 * g + 3}.2", b - 1))
                sp.wait_ge(*full_of(f"s{4 * g + 3}.3", b - 1))
                for s, part in enumerate(SLOTS_K):
                    heads = t["k_parts"][b, part, g // 2].rearrange("(h d) n -> d h n", d=HD)
                    sp.dma_start(KS[HD * s:HD * s + HD, 4 * g:4 * g + 4, :],
                                 heads[:, 4 * (g % 2):4 * (g % 2) + 4, :]).then_inc(K_in[g], 16)

            def queries_in(b, g):
                sp.wait_ge(Q_out, count(16, b, 16))
                sp.wait_ge(*full_of(f"s{4 * g + 3}.2", b - 1))
                sp.wait_ge(*full_of(f"s{4 * g + 3}.3", b - 1))
                for s, part in enumerate(SLOTS_Q):
                    heads = t["q_parts"][b, part, g // 2].rearrange("(h d) n -> d h n", d=HD)
                    sp.dma_start(QS[HD * s:HD * s + HD, 4 * g:4 * g + 4, :],
                                 heads[:, 4 * (g % 2):4 * (g % 2) + 4, :]).then_inc(Q_in[g], 16)

            for s in STEPS:
                r, o, b, f = stages(s)
                if b is not None:
                    keys_in(b, NG - 1)
                    queries_in(b, NG - 1)
                if o is not None and b is not None:
                    sp.wait_ge(*full_of("V1", b))
                    sp.dma_start(cT[:, :, :], t["cT"][o]).then_inc(cT_in, 16)
                if r is not None:
                    sp.wait_ge(v_lo, count(1, r, 1))
                    sp.dma_start(t["v_parts"][r].rearrange("s t p n -> p s t n"), parts[:, :, :, :]).then_inc(v_out, 16)
                    sp.wait_ge(v_out, count(16, r, 16))
                    sp.wait_ge(*full_of(f"vb{DV - 1}", r - 1))
                    sp.wait_ge(*full_of(f"vb{DV - 2}", r - 1))
                    for p in range(3):
                        sp.dma_start(VB[H * p:H * p + H, :, :],
                                     t["v_parts"][r, p].rearrange("t (h e) n -> (t h) e n", e=DV)).then_inc(v_in, 16)
                if r is not None and r + 1 < B:
                    sp.wait_ge(*full_of("gz1", r))
                    sp.dma_start(xT[:, :, :], t["xT"][r + 1]).then_inc(xT_in, 16)
                if o is not None:
                    sp.wait_ge(K_lo, count(1, o, 1))
                    sp.dma_start(t["k_parts"][o].rearrange("s t p n -> p s t n"), parts[:, :, :, :]).then_inc(K_out, 16)
                    keys_in(o, 0)
                    if o + 1 < B:
                        sp.wait_ge(x1_done, count(NT, o, NT))
                        sp.dma_start(xtok[:, :, :], xtok_v[o + 1]).then_inc(xt_in, 16)
                if o is not None:
                    keys_in(o, 1)
                    sp.wait_ge(Q_lo, count(1, o, 1))
                    sp.dma_start(t["q_parts"][o].rearrange("s t p n -> p s t n"), parts[:, :, :, :]).then_inc(Q_out, 16)
                    queries_in(o, 0)
                    queries_in(o, 1)
                if f is not None:
                    sp.wait_ge(x3_done, count(NT, f, NT))
                    sp.dma_start(out_v[f], y3[:, :, :]).then_inc(o_out, 16)
                if o is not None:
                    keys_in(o, 2)
                    queries_in(o, 2)
            sp.wait_ge(o_out, 16 * B + FIRST)
            sp.wait_ge(v_out, 16 * B + FIRST)
            sp.wait_ge(K_out, 16 * B + FIRST)
            sp.wait_ge(Q_out, 16 * B + FIRST)

        @block.tensor
        def _(pe):
            pe.wait_ge(w_in, W_ALL)
            pe.wait_ge(cst, CST)

            def project(out, w_of, x_of):
                for k in range(ND):
                    ins = pe.matmul(out, w_of(k), x_of(k), start=(k == 0), stop=(k == ND - 1))
                return ins

            def by_feature(name, b, w, m, x):
                pe.wait_ge(*free_for(name, b))
                project(bank(name)[:, :], lambda k: w[:, k, m * P:(m + 1) * P], lambda k: x[:, k, :]).then_inc(filled(name), 1)

            def by_token(name, b, x, w, m, tiles=ND):
                pe.wait_ge(*free_for(name, b))
                for half in range(2):
                    tt = 2 * m + half
                    for k in range(tiles):
                        ins = pe.matmul(bank(name)[:, half * D:(half + 1) * D], x[:, k, tt * P:(tt + 1) * P],
                                        w[:, k, :], start=(k == 0), stop=(k == tiles - 1))
                ins.then_inc(filled(name), 1)

            def turn(name, b, x, m):
                pe.wait_ge(*free_for(name, b))
                for tt in range(NT):
                    ins = pe.transpose(bank(name)[:, tt * P:(tt + 1) * P], x[:, tt, m * P:(m + 1) * P], ident[:, :])
                ins.then_inc(filled(name), 1)

            def broadcast_value(a, e):
                if e == 0:
                    pe.wait_ge(v_in, count(48, a, 48))
                pe.wait_ge(*free_for(f"vb{e}", a))
                pe.matmul(bank(f"vb{e}")[:, :], vsel[:, :], VB[:, e, :], start=True, stop=True).then_inc(filled(f"vb{e}"), 1)

            def reduce_step(a, e):
                g, j, i = e // 8, (e % 8) // 2, e % 2
                pe.wait_ge(p_done, count(DV, a, e + 1))
                if e % 8 == 0:
                    pe.wait_ge(*free_for(f"o{g}", a))
                pe.matmul(bank(f"o{g}")[32 * j:32 * j + 32, :], hsel[:, i, :], Pq[:, e % 2, :],
                          start=(i == 0), stop=(i == 1)).then_inc(r_done, 1)

            def max_rows(b, g):
                pe.wait_ge(m_parts, count(NG, b, g + 1))
                pe.wait_ge(*free_for(f"mr{g}", b))
                pe.transpose(bank(f"mr{g}")[:, 0:P // 2].bitcast(BF16),
                             MP[:, :, :].rearrange("p s n -> p (s n)"), identb[:, :]).then_inc(filled(f"mr{g}"), 1)

            def max_tile(b, h, i):
                if h % 4 == 0 and i == 0:
                    pe.wait_ge(K_in[h // 4], count(96, b, 96))
                    pe.wait_ge(Q_in[h // 4], count(96, b, 96))
                n = f"m{h}.{i}"
                pe.wait_ge(*free_for(n, b))
                pe.matmul(bank(n)[:, :], QS[0:NS, h, i * P:(i + 1) * P], KS[0:NS, h, :],
                          start=True, stop=True).then_inc(filled(n), 1)

            def score_tile(b, h, i):
                if i == 0 and h % 4 == 0:
                    pe.wait_ge(m_in, count(48 * NG, b, 48 * (h // 4 + 1)))
                n = f"s{h}.{i}"
                pe.wait_ge(*free_for(n, b))
                pe.matmul(bank(n)[:, :], KS[0:NR, h, i * P:(i + 1) * P], QS[0:NR, h, :],
                          start=True, stop=True).then_inc(filled(n), 1)

            def value_tile(b, h, i):
                g, j = h // 4, h % 4
                pe.wait_ge(*read(f"s{h}.{i}", b))
                if h == 0 and i == 0:
                    pe.wait_ge(*read("V0", b))
                    pe.wait_ge(*read("V1", b))
                if j == 0 and i == 0:
                    pe.wait_ge(*free_for(f"pv{g}", b))
                ins = pe.matmul(bank(f"pv{g}")[32 * j:32 * j + 32, :], Vs[:, i, h, :], PT[:, h % 2, i, :],
                                start=(i == 0), stop=(i == NT - 1))
                if i == NT - 1:
                    ins.then_inc(pv_done, 1)

            def projecting(r, at):
                if at == (1, 0):
                    pe.wait_ge(xT_in, count(16, r, 16))
                    by_feature("gv0", r, wv, 0, xT)
                if at == (1, 1):
                    by_feature("gv1", r, wv, 1, xT)
                if at == (1, 3):
                    pe.wait_ge(*free_for("gg1", r))
                    project(bank("gg1")[0:16, :], lambda k: wg1[:, k, :], lambda k: xT[:, k, :]).then_inc(filled("gg1"), 1)
                if at == (2, 3):
                    pe.wait_ge(*read("gg1", r))
                    pe.wait_ge(*free_for("gg", r))
                    pe.matmul(bank("gg")[:, :], wg2[:, :], kg1[:, :], start=True, stop=True).then_inc(filled("gg"), 1)
                if at == (3, 0):
                    by_feature("gq", r, wq, 0, xT)
                if at == (3, 1):
                    by_feature("gk", r, wk, 0, xT)
                if at == (5, 0):
                    by_feature("gz0", r, wg, 0, xT)
                if at == (5, 1):
                    by_feature("gz1", r, wg, 1, xT)
                n, i = at
                if n >= 8 and i % 2 == 0:
                    broadcast_value(r, 2 * (n - 8) + i // 2)
                if n >= 9 and i % 2 == 1:
                    reduce_step(r, 2 * (n - 9) + i // 2)

            def gated_end(o, at):
                if at == (0, 0):
                    reduce_step(o, DV - 2)
                if at == (0, 1):
                    reduce_step(o, DV - 1)
                if at == (1, 2):
                    pe.wait_ge(*read("o0", o))
                    pe.wait_ge(*read("o1", o))
                    pe.wait_ge(*free_for("mean", o))
                    project(bank("mean")[:, :], lambda k: mavg[:, :], lambda k: oS[:, k, :]).then_inc(filled("mean"), 1)
                if at == (2, 2):
                    pe.wait_ge(o_sq, count(1, o, 1))
                    pe.wait_ge(*free_for("var", o))
                    project(bank("var")[:, :], lambda k: mavg[:, :], lambda k: sq[:, k, :]).then_inc(filled("var"), 1)
                if at == (3, 2):
                    pe.wait_ge(w2_in, W2_ALL)
                    pe.wait_ge(cT_in, count(16, o, 16))
                    by_feature("K0", o, xwk, 0, cT)
                if at == (3, 3):
                    by_feature("K1", o, xwk, 1, cT)
                if at == (4, 2):
                    pe.wait_ge(gated, count(1, o, 1))
                    by_token("gy0", o, oS, wo, 0)
                if at == (4, 3):
                    by_token("gy1", o, oS, wo, 1)
                if at == (6, 0):
                    pe.wait_ge(x1_done, count(NT, o, NT))
                    turn("gt0", o, x1, 0)
                if at == (6, 1):
                    turn("gt1", o, x1, 1)
                if at == (7, 0):
                    pe.wait_ge(*read("gt0", o))
                    pe.wait_ge(*read("gt1", o))
                    by_feature("Q0", o, xwq, 0, x1T)
                if at == (7, 1):
                    by_feature("Q1", o, xwq, 1, x1T)

            def feed_forward(f, at):
                if at == (2, 0):
                    pe.wait_ge(normal, count(NG, f, NG))
                    by_token("y0", f, OT, xwo, 0, NG)
                if at == (2, 1):
                    by_token("y1", f, OT, xwo, 1, NG)
                if at == (4, 0):
                    pe.wait_ge(x2_done, count(NT, f, NT))
                    turn("t0", f, x2, 0)
                if at == (4, 1):
                    turn("t1", f, x2, 1)
                if at == (5, 2):
                    pe.wait_ge(mix_done, count(2, f, 1))
                    by_token("r0", f, xr, fwr, 0)
                if at == (5, 3):
                    by_token("r1", f, xr, fwr, 1)
                if at == (6, 2):
                    pe.wait_ge(mix_done, count(2, f, 2))
                    by_feature("f0", f, fwk, 0, xk)
                if at == (6, 3):
                    by_feature("f1", f, fwk, 1, xk)
                if at == (8, 1):
                    pe.wait_ge(ka2, count(1, f, 1))
                    by_token("w0", f, ka, fwv, 0)
                if at == (8, 3):
                    by_token("w1", f, ka, fwv, 1)

            for s in STEPS:
                r, o, b, f = stages(s)
                for n in range(H):
                    for i in range(NT):
                        if b is not None:
                            score_tile(b, n, i)
                        if r is not None:
                            projecting(r, (n, i))
                        if o is not None:
                            gated_end(o, (n, i))
                        if f is not None:
                            feed_forward(f, (n, i))
                        if b is not None and n == 0 and i < 2:
                            by_token(f"V{i}", b, cT, xwv, i)
                        if n % 4 == 3 and i == 1 and n < H - 1 and b is not None:
                            max_rows(b, (n + 1) // 4)
                        if n == H - 1 and i == 1 and o is not None:
                            max_rows(o, 0)
                        if n + LAG < H and b is not None:
                            max_tile(b, n + LAG, i)
                        if n + LAG >= H and o is not None:
                            max_tile(o, n + LAG - H, i)
                        if n >= 1 and b is not None:
                            value_tile(b, n - 1, i)
                        if n == 0 and f is not None:
                            value_tile(f, H - 1, i)

        @block.scalar
        def _(act):
            act.preload_act_table_set("natural_log_exp_and_others")
            act.wait_ge(w_in, W_ALL)
            act.wait_ge(cst, CST)

            def projecting(r, at):
                if at in ((1, 2), (1, 3)):
                    m = at[1] - 2
                    act.wait_ge(*full_of(f"gv{m}", r))
                    if m == 0:
                        act.wait_ge(Q_lo, count(1, r - 2, 1) if r >= 2 else FIRST)
                    act.activation(full32[:, m, :], bank(f"gv{m}")[:, :], ACT.Copy).then_inc(emptied(f"gv{m}"), 1)
                if at == (1, 3):
                    act.wait_ge(*read("gv0", r))
                    act.wait_ge(*read("gv1", r))
                    act.wait_ge(Q_out, count(16, r - 2, 16) if r >= 2 else FIRST)
                    act.activation(parts[:, 0, :, :], full32[:, :, :], ACT.Copy).then_inc(v_hi, 1)
                if at == (2, 0):
                    act.wait_ge(*full_of("gg1", r))
                    act.activation(kg1[:, :], bank("gg1")[0:16, :], ACT.Copy).then_inc(emptied("gg1"), 1)
                if at == (2, 3):
                    act.wait_ge(v_r1, count(1, r, 1))
                    act.activation(parts[:, 1, :, :], full32[:, :, :], ACT.Copy).then_inc(v_mid, 1)
                if at == (3, 1):
                    act.wait_ge(*full_of("gg", r))
                    act.activation(kz[:, 0, :], bank("gg")[:, :], ACT.Copy).then_inc(emptied("gg"), 1)
                if at == (3, 2):
                    act.wait_ge(*full_of("gq", r))
                    act.wait_ge(p_done, count(DV, r, 0))
                    act.activation(qT[:, :], bank("gq")[:, :], ACT.Copy).then_inc(emptied("gq"), 1)
                if at == (3, 3):
                    act.wait_ge(*full_of("gk", r))
                    act.wait_ge(s_done, count(DV, r, 0))
                    act.activation(kT[:, :], bank("gk")[:, :], ACT.Copy, scale=float(DK) ** -0.5).then_inc(emptied("gk"), 1)
                if at in ((5, 2), (5, 3)):
                    m = at[1] - 2
                    act.wait_ge(*full_of(f"gz{m}", r))
                    act.wait_ge(o_gate, count(1, r, 0))
                    act.activation(kz[:, 1 + m, :], bank(f"gz{m}")[:, :], ACT.Identity,
                                   bias=bg[:, m:m + 1]).then_inc(emptied(f"gz{m}"), 1)
                if at == (6, 3):
                    act.wait_ge(*read("gg", r))
                    act.wait_ge(*read("gz0", r))
                    act.wait_ge(*read("gz1", r))
                    act.wait_ge(gated, count(1, r, 0))
                    act.activation(ab[:, :, :], kz[:, :, :], ACT.Abs).then_inc(kz_abs, 1)
                if at == (7, 0):
                    act.wait_ge(kz_abs, count(1, r, 1))
                    act.activation(ab[:, :, :], ab[:, :, :], ACT.Exp, scale=-1.0).then_inc(kz_exp, 1)
                if at == (7, 1):
                    act.wait_ge(kz_exp, count(1, r, 1))
                    act.activation(ab[:, :, :], ab[:, :, :], ACT.Ln, bias=one[:, :]).then_inc(kz_ln, 1)
                if at == (7, 3):
                    act.wait_ge(kz_ls, count(1, r, 1))
                    act.activation(ab[:, 0, :], ab[:, 0, :], ACT.Exp, scale=1.0 / 16.0).then_inc(kz_sig, 1)
                    act.activation(ab[:, 1:3, :], ab[:, 1:3, :], ACT.Exp).then_inc(kz_sig, 1)
                if at == (13, 0):
                    act.wait_ge(r_done, count(DV, r, 8))
                    act.activation(oS[:, 0, :], bank("o0")[:, :], ACT.Copy).then_inc(emptied("o0"), 1)

            def gated_end(o, at):
                if at == (0, 2):
                    act.wait_ge(r_done, count(DV, o, DV))
                    act.activation(oS[:, 1, :], bank("o1")[:, :], ACT.Copy).then_inc(emptied("o1"), 1)
                if at == (2, 1):
                    act.wait_ge(*read("mean", o))
                    act.activation(sq[:, :, :], oS[:, :, :], ACT.Square).then_inc(o_sq, 1)
                if at == (3, 0):
                    act.wait_ge(*full_of("var", o))
                    act.wait_ge(gate_z, count(1, o, 1))
                    act.activation(rsd, bank("var")[:, :], ACT.Ln, bias=eps[:, :]).then_inc(emptied("var"), 1)
                    act.wait_ge(*read("var", o))
                    act.activation(rsd, rsd, ACT.Exp, scale=-0.5).then_inc(o_rs, 1)
                if at == (4, 0):
                    for m in range(ND):
                        act.wait_ge(*full_of(f"K{m}", o))
                        act.wait_ge(v_lo, count(1, min(o + 1, B - 1), 1))
                        act.activation(full32[:, m, :], bank(f"K{m}")[:, :], ACT.Copy).then_inc(emptied(f"K{m}"), 1)
                    act.wait_ge(*read("K0", o))
                    act.wait_ge(*read("K1", o))
                    act.wait_ge(v_out, count(16, min(o + 1, B - 1), 16))
                    act.wait_ge(Q_out, count(16, o, 0))
                    act.activation(parts[:, 0, :, :], full32[:, :, :], ACT.Copy).then_inc(K_hi, 1)
                if at == (5, 0):
                    act.wait_ge(K_r1, count(1, o, 1))
                    act.activation(parts[:, 1, :, :], full32[:, :, :], ACT.Copy).then_inc(K_mid, 1)
                if at == (6, 2):
                    for m in range(ND):
                        act.wait_ge(*full_of(f"gt{m}", o))
                        act.wait_ge(*full_of("Q1", o - 1))
                        act.activation(x1T[:, m, :], bank(f"gt{m}")[:, :], ACT.Copy).then_inc(emptied(f"gt{m}"), 1)
                if at == (7, 2):
                    for m in range(ND):
                        act.wait_ge(*full_of(f"Q{m}", o))
                        act.wait_ge(K_lo, count(1, o, 1))
                        act.activation(full32[:, m, :], bank(f"Q{m}")[:, :], ACT.Copy,
                                       scale=float(HD) ** -0.5).then_inc(emptied(f"Q{m}"), 1)
                    act.wait_ge(*read("Q0", o))
                    act.wait_ge(*read("Q1", o))
                    act.wait_ge(K_out, count(16, o, 16))
                    act.activation(parts[:, 0, :, :], full32[:, :, :], ACT.Copy).then_inc(Q_hi, 1)
                if at == (8, 1):
                    act.wait_ge(Q_r1, count(1, o, 1))
                    act.activation(parts[:, 1, :, :], full32[:, :, :], ACT.Copy).then_inc(Q_mid, 1)

            def feed_forward(f, at):
                if at == (4, 2):
                    for m in range(ND):
                        act.wait_ge(*full_of(f"t{m}", f))
                        act.wait_ge(mix_done, count(2, f, 0))
                        act.activation(x2T[:, m, 1:S + 1], bank(f"t{m}")[:, :], ACT.Copy).then_inc(emptied(f"t{m}"), 1)
                if at == (6, 0):
                    for m in range(2):
                        act.wait_ge(*full_of(f"r{m}", f))
                        act.wait_ge(o_out, count(16, f, 0))
                        act.activation(rl[:, 2 * m:2 * m + 2, :], tokens(f"r{m}"), ACT.Copy).then_inc(emptied(f"r{m}"), 1)
                    act.wait_ge(*read("r0", f))
                    act.wait_ge(*read("r1", f))
                    act.wait_ge(x3_done, count(NT, f, 0))
                    act.activation(ra[:, :, :], rl[:, :, :], ACT.Abs).then_inc(r_abs, 1)
                if at == (6, 1):
                    act.wait_ge(r_abs, count(1, f, 1))
                    act.activation(ra[:, :, :], ra[:, :, :], ACT.Exp, scale=-1.0).then_inc(r_exp, 1)
                if at == (6, 2):
                    act.wait_ge(r_exp, count(1, f, 1))
                    act.activation(ra[:, :, :], ra[:, :, :], ACT.Ln, bias=one[:, :]).then_inc(r_ln, 1)
                if at == (7, 0):
                    for m in range(ND):
                        act.wait_ge(*full_of(f"f{m}", f))
                        act.wait_ge(*full_of("w1", f - 1))
                        act.activation(ka[:, m, :], bank(f"f{m}")[:, :], ACT.Relu).then_inc(emptied(f"f{m}"), 1)
                if at == (7, 1):
                    act.wait_ge(r_ls, count(1, f, 1))
                    act.activation(ra[:, :, :], ra[:, :, :], ACT.Exp).then_inc(r_sig, 1)

            def max_rows(b, g):
                act.wait_ge(*full_of(f"mr{g}", b))
                act.wait_ge(m_in, count(48 * NG, b, 48 * g))
                act.activation(mrow[:, :], bank(f"mr{g}")[0:48, 0:P // 2].bitcast(BF16), ACT.Copy).then_inc(emptied(f"mr{g}"), 1)
                act.wait_ge(*read(f"mr{g}", b))
                for p in range(3):
                    act.dma_start(QS[NS + p:NS + p + 1, 4 * g:4 * g + 4, :], mrow[16 * p:16 * p + 16, :]).then_inc(m_in, 16)

            def exp_tile(b, h, i):
                n = f"s{h}.{i}"
                act.wait_ge(*full_of(n, b))
                if i == 0:
                    act.wait_ge(pv_done, FIRST + max(H * b + h - 1, 0))
                act.activation(PT[:, h % 2, i, :], bank(n)[:, :], ACT.Exp).then_inc(emptied(n), 1)

            def unload(b, g):
                act.wait_ge(pv_done, count(H, b, 4 * (g + 1)))
                act.wait_ge(*full_of("y1", b - 1))
                act.activation(OT[:, g, :], bank(f"pv{g}")[:, :], ACT.Copy).then_inc(emptied(f"pv{g}"), 1)

            def invert(b, g):
                act.wait_ge(d_sh, count(NG, b, g + 1))
                act.activation(den[:, :], den[:, :], ACT.Ln).then_inc(d_ln, 1)
                act.wait_ge(d_ln, count(NG, b, g + 1))
                act.activation(den[:, :], den[:, :], ACT.Exp, scale=-1.0).then_inc(d_inv, 1)

            for s in STEPS:
                r, o, b, f = stages(s)
                for n in range(H):
                    group = ((f, NG - 1) if n == 1 else (b, n // 4 - 1)) if n % 4 == 1 else (None, None)
                    for i in range(NT):
                        if i == 0 and group[0] is not None:
                            unload(*group)
                        if r is not None:
                            projecting(r, (n, i))
                        if f is not None:
                            feed_forward(f, (n, i))
                        if o is not None:
                            gated_end(o, (n, i))
                        if b is not None:
                            exp_tile(b, n, i)
                        if n % 4 == 3 and i == 1 and n < H - 1 and b is not None:
                            max_rows(b, (n + 1) // 4)
                        if n == H - 1 and i == 1 and o is not None:
                            max_rows(o, 0)
                        if i == 2 and group[0] is not None:
                            invert(*group)
                        if n == 0 and i == 3 and b is not None:
                            for m in range(2):
                                act.wait_ge(*full_of(f"V{m}", b))
                                act.wait_ge(pv_done, count(H, b, 0))
                                act.activation(Vs[:, 2 * m:2 * m + 2, :, 0:HD],
                                               bank(f"V{m}")[:, :].rearrange("p (t h e) -> p t h e", t=2, e=HD),
                                               ACT.Copy).then_inc(emptied(f"V{m}"), 1)

        @block.vector
        def _(dve):
            dve.memset(eps[:, :], EPS).then_inc(cst, 1)
            dve.memset(eps4[:, :], EPS).then_inc(cst, 1)
            dve.memset(zero[:, :], 0.0).then_inc(cst, 1)
            dve.memset(MP[:, :, :], 0.0).then_inc(cst, 1)
            dve.memset(one[:, :], 1.0).then_inc(cst, 1)
            dve.memset(x2T[:, :, 0:1], 0.0).then_inc(cst, 1)
            dve.wait_ge(w_in, W_ALL)
            dve.tensor_copy(vsel[:, :], vsel32[:, :]).then_inc(cst, 1)
            dve.tensor_copy(identb[:, :], ident[:, :]).then_inc(cst, 1)
            dve.tensor_scalar(omr[:, :], mur[:, :], -1.0, 1.0, ALU.mult, ALU.add).then_inc(cst, 1)
            dve.tensor_scalar(omk[:, :], muk[:, :], -1.0, 1.0, ALU.mult, ALU.add).then_inc(cst, 1)
            dve.memset(Vs[:, :, :, HD:HD + 1], 1.0).then_inc(ks_set, 1)
            dve.memset(Vs[:, :, :, HD + 1:32], 0.0).then_inc(ks_set, 1)
            dve.memset(KS[NS:NR, :, :], -1.0).then_inc(ks_set, 1)
            dve.wait_ge(cst, CST)

            def statistics(n, src, b):
                for tt in range(NT):
                    ins = dve.bn_stats(st[n][:, tt, :], src[:, tt, :])
                ins.then_inc(st_done[n], 1)
                dve.wait_ge(st_done[n], count(1, b, 1))
                for tt in range(NT):
                    ins = dve.bn_aggr(mv[n][:, tt, :], st[n][:, tt, :])
                ins.then_inc(mv_done[n], 1)

            def norm(n, src, dst, done, b):
                dve.wait_ge(rs_done[n], count(1, b, 1))
                for tt in range(NT):
                    dve.tensor_scalar(dst[:, tt, :], src[:, tt, :], mv[n][:, tt, 0:1], rs[n][:, tt:tt + 1],
                                      ALU.subtract, ALU.mult).then_inc(done, 1)

            def projecting(r, at):
                if at == (7, 2):
                    dve.wait_ge(kz_ln, count(1, r, 1))
                    dve.scalar_tensor_tensor(ab[:, :, :], kz[:, :, :], 0.0, ab[:, :, :], ALU.min, ALU.subtract)\
                       .then_inc(kz_ls, 1)
                n, i = at
                if n >= 8:
                    e = 2 * (n - 8) + i // 2
                    if i % 2 == 0:
                        dve.wait_ge(*full_of(f"vb{e}", r))
                        if e == 0:
                            dve.wait_ge(*read("gk", r))
                        dve.tensor_tensor(U[:, e % 2, :], kT[:, :], bank(f"vb{e}")[:, :], ALU.mult).then_inc(emptied(f"vb{e}"), 1)
                    else:
                        dve.wait_ge(*read(f"vb{e}", r))
                        if e == 1 or e == 0:
                            dve.wait_ge(kz_sig, count(2, r, 1))
                        dve.wait_ge(p_done, count(DV, r, max(e - 1, 0)))
                        dve.tensor_tensor_scan(St[:, e % 2, :], ab[:, 0, :], U[:, e % 2, :], 0.0, ALU.mult, ALU.add)\
                           .then_inc(s_done, 1)

            def gated_end(o, at):
                if at == (2, 0):
                    dve.wait_ge(*full_of("mean", o))
                    for g in range(ND):
                        ins = dve.tensor_tensor(oS[:, g, :], oS[:, g, :], bank("mean")[:, :], ALU.subtract)
                    ins.then_inc(emptied("mean"), 1)
                if at == (5, 0):
                    for m in range(2):
                        dve.wait_ge(*full_of(f"gy{m}", o))
                        if m == 0:
                            dve.wait_ge(xt_in, count(16, o, 16))
                        dve.tensor_tensor(xtok[:, 2 * m:2 * m + 2, :], tokens(f"gy{m}"),
                                          xtok[:, 2 * m:2 * m + 2, :], ALU.add).then_inc(emptied(f"gy{m}"), 1)
                    dve.wait_ge(*read("gy0", o))
                    dve.wait_ge(*read("gy1", o))
                    statistics(0, xtok, o)
                if at == (5, 2):
                    dve.wait_ge(x1b_done, count(1, o, 0))
                    dve.wait_ge(*full_of("gt1", o - 1))
                    norm(0, xtok, x1, x1_done, o)

            def feed_forward(f, at):
                xb = x1b[:, (f or 0) % 2, :, :]
                if at == (2, 2):
                    for m in range(2):
                        dve.wait_ge(*full_of(f"y{m}", f))
                        if m == 0:
                            dve.wait_ge(x1b_done, count(1, f, 1))
                        dve.tensor_tensor(xb[:, 2 * m:2 * m + 2, :], tokens(f"y{m}"),
                                          xb[:, 2 * m:2 * m + 2, :], ALU.add).then_inc(emptied(f"y{m}"), 1)
                if at == (2, 3):
                    dve.wait_ge(*read("y0", f))
                    dve.wait_ge(*read("y1", f))
                    statistics(1, xb, f)
                if at == (3, 1):
                    dve.wait_ge(*full_of("t1", f - 1))
                    dve.wait_ge(x3_done, count(NT, f, 0))
                    norm(1, xb, x2, x2_done, f)
                if at in ((5, 1), (5, 3)):
                    which = at[1] // 2
                    mu, dst = ((mur, xr), (muk, xk))[which]
                    dve.wait_ge(mix_p, count(2, f, which + 1))
                    for m in range(ND):
                        ins = dve.scalar_tensor_tensor(dst[:, m, :], x2T[:, m, 1:S + 1], mu[:, m:m + 1], dst[:, m, :],
                                                       ALU.mult, ALU.add)
                    ins.then_inc(mix_done, 1)
                if at == (6, 3):
                    dve.wait_ge(r_ln, count(1, f, 1))
                    dve.scalar_tensor_tensor(ra[:, :, :], rl[:, :, :], 0.0, ra[:, :, :], ALU.min, ALU.subtract)\
                       .then_inc(r_ls, 1)
                if at in ((8, 2), (9, 0)):
                    m = at[0] - 8
                    dve.wait_ge(r_sig, count(1, f, 1))
                    dve.wait_ge(*full_of(f"w{m}", f))
                    dve.tensor_tensor(ra[:, 2 * m:2 * m + 2, :], tokens(f"w{m}"),
                                      ra[:, 2 * m:2 * m + 2, :], ALU.mult).then_inc(emptied(f"w{m}"), 1)
                if at == (9, 1):
                    dve.wait_ge(*read("w1", f))
                    dve.tensor_tensor(ra[:, :, :], ra[:, :, :], x2[:, :, :], ALU.add).then_inc(f_mul, 1)
                if at == (9, 2):
                    dve.wait_ge(f_mul, count(1, f, 1))
                    statistics(2, ra, f)
                if at == (10, 1):
                    norm(2, ra, y3, x3_done, f)

            def max_tile(b, h, i):
                n = f"m{h}.{i}"
                dve.wait_ge(*full_of(n, b))
                if h % 4 == 0 and i == 0:
                    dve.wait_ge(m_parts, count(NG, b - 1, h // 4 + 1) if b else FIRST)
                dve.tensor_reduce(MX[:, NT * h + i:NT * h + i + 1], bank(n)[:, :], AX.X, ALU.max).then_inc(emptied(n), 1)

            def spread(b, g):
                dve.wait_ge(*read(f"pv{g}", b))
                dve.wait_ge(normal, count(NG, b, g))
                dve.stream_shuffle(den[:, :], OT[:, g, :], [HD] * 32).then_inc(d_sh, 1)

            def normalise(b, g):
                dve.wait_ge(d_inv, count(NG, b, g + 1))
                dve.tensor_tensor(OT[:, g, :], OT[:, g, :], den[:, :], ALU.mult).then_inc(normal, 1)

            for s in STEPS:
                r, o, b, f = stages(s)
                for n in range(H):
                    group = ((f, NG - 1) if n == 1 else (b, n // 4 - 1)) if n % 4 == 1 else (None, None)
                    for i in range(NT):
                        if f is not None:
                            feed_forward(f, (n, i))
                        if o is not None:
                            gated_end(o, (n, i))
                        if r is not None:
                            projecting(r, (n, i))
                        if n + LAG < H and b is not None:
                            max_tile(b, n + LAG, i)
                        if n + LAG >= H and o is not None:
                            max_tile(o, n + LAG - H, i)
                        if group[0] is not None and i == 1:
                            spread(*group)
                        if group[0] is not None and i == 3:
                            normalise(*group)

        @block.gpsimd
        def _(pool):
            pool.memset(mhalf[:, :], -0.5).then_inc(cst, 1)
            pool.wait_ge(w_in, W_ALL)
            pool.wait_ge(cst, CST)

            def first_rest(hi, r1, b):
                pool.wait_ge(hi, count(1, b, 1))
                pool.tensor_tensor(full32[:, :, :], full32[:, :, :], parts[:, 0, :, :], ALU.subtract).then_inc(r1, 1)

            def second_rest(mid, lo, b):
                pool.wait_ge(mid, count(1, b, 1))
                pool.tensor_tensor(parts[:, 2, :, :], full32[:, :, :], parts[:, 1, :, :], ALU.subtract).then_inc(lo, 1)

            def inverse_deviation(n, b):
                pool.wait_ge(mv_done[n], count(1, b, 1))
                pool.tensor_tensor(rs[n][:, :], mv[n][:, :, 1], eps4[:, :], ALU.add).then_inc(ve_done[n], 1)
                pool.wait_ge(ve_done[n], count(1, b, 1))
                pool.tensor_tensor(rs[n][:, :], rs[n][:, :], mhalf[:, :], ALU.pow).then_inc(rs_done[n], 1)

            def projecting(r, at):
                if at == (1, 3):
                    first_rest(v_hi, v_r1, r)
                if at == (2, 3):
                    second_rest(v_mid, v_lo, r)
                if at == (9, 0):
                    pool.wait_ge(kz_sig, count(2, r, 2))
                    pool.tensor_tensor(kz[:, 1:3, :], kz[:, 1:3, :], ab[:, 1:3, :], ALU.mult).then_inc(gate_z, 1)
                n, i = at
                if n >= 8 and i % 2 == 1:
                    e = 2 * (n - 8) + i // 2
                    pool.wait_ge(s_done, count(DV, r, e + 1))
                    if e == 0:
                        pool.wait_ge(*read("gq", r))
                    pool.wait_ge(r_done, count(DV, r, max(e - 1, 0)))
                    pool.tensor_tensor(Pq[:, e % 2, :], qT[:, :], St[:, e % 2, :], ALU.mult).then_inc(p_done, 1)

            def gated_end(o, at):
                if at == (2, 1):
                    pool.wait_ge(o_sq, count(1, o, 1))
                    pool.wait_ge(gate_z, count(1, o, 1))
                    pool.tensor_tensor(oS[:, :, :], oS[:, :, :], kz[:, 1:3, :], ALU.mult).then_inc(o_gate, 1)
                if at == (3, 1):
                    pool.wait_ge(o_rs, count(1, o, 1))
                    pool.wait_ge(o_gate, count(1, o, 1))
                    pool.tensor_tensor(oS[:, :, :], oS[:, :, :], rsd.unsqueeze(1).broadcast_to([P, ND, S]),
                                       ALU.mult).then_inc(gated, 1)
                if at == (4, 1):
                    first_rest(K_hi, K_r1, o)
                if at == (5, 0):
                    second_rest(K_mid, K_lo, o)
                if at == (5, 1):
                    inverse_deviation(0, o)
                if at == (6, 1):
                    pool.wait_ge(w2_in, W2_ALL)
                    pool.wait_ge(x1_done, count(NT, o, NT))
                    pool.wait_ge(x2_done, count(NT, o - 1, 0) if o else FIRST)
                    pool.tensor_tensor(x1b[:, o % 2, :, :], x1[:, :, :], xbo[:, :].unsqueeze(1).broadcast_to([P, NT, D]),
                                       ALU.add).then_inc(x1b_done, 1)
                if at == (7, 3):
                    first_rest(Q_hi, Q_r1, o)
                if at == (8, 2):
                    second_rest(Q_mid, Q_lo, o)

            def feed_forward(f, at):
                if at == (2, 3):
                    inverse_deviation(1, f)
                if at in ((4, 2), (4, 3)):
                    which = at[1] - 2
                    om, dst, last = ((omr, xr, "r1"), (omk, xk, "f1"))[which]
                    pool.wait_ge(*read("t0", f))
                    pool.wait_ge(*read("t1", f))
                    pool.wait_ge(*full_of(last, f - 1))
                    if which == 0:
                        pool.wait_ge(x3_done, count(NT, f, 0))
                    for m in range(ND):
                        ins = pool.tensor_tensor(dst[:, m, :], x2T[:, m, 0:S], om[:, m:m + 1].broadcast_to([P, S]), ALU.mult)
                    ins.then_inc(mix_p, 1)
                if at == (7, 1):
                    pool.wait_ge(*read("f0", f))
                    pool.wait_ge(*read("f1", f))
                    pool.tensor_tensor(ka[:, :, :], ka[:, :, :], ka[:, :, :], ALU.mult).then_inc(ka2, 1)
                if at == (9, 3):
                    inverse_deviation(2, f)

            def max_parts(b, g):
                pool.wait_ge(*read(f"m{4 * g + 3}.{NT - 2}", b))
                pool.wait_ge(*read(f"m{4 * g + 3}.{NT - 1}", b))
                pool.wait_ge(*full_of(f"mr{(g - 1) % NG}", b if g else b - 1))
                m = MX[:, 16 * g:16 * g + 16]
                ops = [lambda: pool.tensor_tensor(MP[:, 0, :], m, zero[:, :], ALU.add),
                       lambda: pool.tensor_tensor(MR[:, 0, :], m, MP[:, 0, :], ALU.subtract),
                       lambda: pool.tensor_tensor(MP[:, 1, :], MR[:, 0, :], zero[:, :], ALU.add)]
                for k, op in enumerate(ops):
                    op().then_inc(m_step, 1)
                    pool.wait_ge(m_step, count(3 * NG, b, 3 * g + k + 1))
                pool.tensor_tensor(MP[:, 2, :], MR[:, 0, :], MP[:, 1, :], ALU.subtract).then_inc(m_parts, 1)

            for s in STEPS:
                r, o, b, f = stages(s)
                for n in range(H):
                    for i in range(NT):
                        if n % 4 == 2 and i == 3 and n < H - 2 and b is not None:
                            max_parts(b, n // 4 + 1)
                        if n == H - 2 and i == 3 and o is not None:
                            max_parts(o, 0)
                        if f is not None:
                            feed_forward(f, (n, i))
                        if o is not None:
                            gated_end(o, (n, i))
                        if r is not None:
                            projecting(r, (n, i))


def layouts(i):
    import numpy as np

    def rows(w):
        return np.ascontiguousarray(w.reshape(-1, P, w.shape[1]).transpose(1, 0, 2))

    def by_feature(x):
        return np.ascontiguousarray(x.transpose(0, 2, 1).reshape(B, ND, P, S).transpose(0, 2, 1, 3))

    eh = np.arange(D).reshape(H, DV).T.reshape(-1)
    xwo = np.zeros((NG, 4, 32, D), np.float32)
    xwo[:, :, :HD] = i["L0_xattn_W_o"].reshape(NG, 4, HD, D)
    hsel = np.zeros((P, 2, 32), np.float32)
    vsel = np.zeros((3 * H, P), np.float32)
    for r in range(P):
        for s in range(2):
            hsel[r, s, 16 * s + r // DK] = 1
        for s in range(3):
            vsel[H * s + r // DK, r] = 1
    r = np.arange(P)
    mavg = ((r[:, None] % H) == (r[None, :] % H)).astype(np.float32) / DV
    return {
        "x": i["x"], "xT": by_feature(i["x"]), "cT": by_feature(i["ctx_1024"]),
        "wq": rows(i["L0_attn_Wq"]), "wk": rows(i["L0_attn_Wk"]), "wg1": rows(i["L0_attn_Wg1"]),
        "wg2": i["L0_attn_Wg2"], "wv": rows(i["L0_attn_Wv"]),
        "wg": rows(i["L0_attn_Wg"][:, eh]), "bg": np.ascontiguousarray(i["L0_attn_bg"][eh].reshape(ND, P).T),
        "wo": rows(i["L0_attn_Wo"][eh]),
        "xwq": rows(i["L0_xattn_W_q"]), "xwk": rows(i["L0_xattn_W_k"]), "xwv": rows(i["L0_xattn_W_v"]),
        "xwo": np.ascontiguousarray(xwo.reshape(NG, P, D).transpose(1, 0, 2)), "xbo": i["L0_xattn_b_o"],
        "fwr": rows(i["L0_ffn_W_r"].T), "fwk": rows(i["L0_ffn_W_k"].T), "fwv": rows(i["L0_ffn_W_v"].T),
        "mur": np.ascontiguousarray(i["L0_ffn_mu_r"].reshape(ND, P).T),
        "muk": np.ascontiguousarray(i["L0_ffn_mu_k"].reshape(ND, P).T),
        "hsel": hsel, "vsel": vsel, "mavg": mavg,
        "ident": np.eye(P, dtype=np.float32),
    }


def kernel(**inputs):
    import numpy as np
    import concourse.bacc as bacc
    from concourse.bass_utils import run_bass_kernel_spmd

    nc = bacc.Bacc("TRN2", target_bir_lowering=False, num_devices=1)
    arrays, t = {}, {}
    for name, a in layouts({k: np.asarray(v) for k, v in inputs.items()}).items():
        arrays[f"in_{name}"] = np.ascontiguousarray(a)
        t[name] = nc.dram_tensor(f"in_{name}", a.shape, mybir.dt.from_np(a.dtype), kind="ExternalInput").ap()
    for name in ("v_parts", "k_parts", "q_parts"):
        t[name] = nc.dram_tensor(name, (B, 3, ND, P, S), BF16, kind="Internal").ap()
    t["out"] = nc.dram_tensor("out_0", (B, S, D), F32, kind="ExternalOutput").ap()
    build(nc, t)
    r = run_bass_kernel_spmd(nc, [arrays], core_ids=[0])
    return r.results[0]["out_0"]
```

```python
from contextlib import ExitStack

import concourse.bass as bass
from concourse import mybir

ALU = mybir.AluOpType
ACT = mybir.ActivationFunctionType
F32 = mybir.dt.float32
BF16 = mybir.dt.bfloat16
AX = mybir.AxisListType

P = 128
B, S, D = 4, 512, 256
H = 16
DK, DV = 8, 16
HD = 16
ND = D // P
NT = S // P
NG = H // 4
EPS = 1e-5
LAG = 5
SLOTS_K = [0, 0, 1, 1, 0, 2]
SLOTS_Q = [0, 1, 0, 1, 2, 0]
NS = 16 * len(SLOTS_K)
NR = NS + 3

STEPS = range(-2, B + 2)


def stages(s):
    return [x if 0 <= x < B else None for x in (s + 2, s + 1, s, s - 1, s - 2)]


SIDE_USES = {
    (0, 0): ("V0", "b", 2), (0, 1): ("V1", "b", 1),
    (1, 0): ("gv0", "r", 0), (1, 1): ("gv1", "r", 2), (1, 2): ("mean", "o", 1), (1, 3): ("gg1", "r", 0),
    (2, 0): ("y0", "f", 2), (2, 1): ("y1", "f", 1), (2, 2): ("var", "o", 0), (2, 3): ("gg", "r", 2),
    (3, 0): ("gq", "r", 1), (3, 1): ("gk", "r", 0), (3, 2): ("K0", "o", 2), (3, 3): ("K1", "o", 1),
    (4, 0): ("t0", "f", 0), (4, 1): ("t1", "f", 2), (4, 2): ("gy0", "o", 1), (4, 3): ("gy1", "o", 0),
    (5, 3): ("r0", "f", 1), (6, 0): ("gt0", "o", 0), (6, 1): ("gt1", "o", 2), (6, 2): ("r1", "f", 1),
    (7, 0): ("Q0", "o", 2), (7, 1): ("Q1", "o", 0), (8, 1): ("f0", "f", 0), (8, 3): ("f1", "f", 1),
    (11, 3): ("w0", "f", 1), (12, 3): ("w1", "f", 1),
}


def gate_slot(r):
    return 10 if r >= 2 else 9


def scan_slot(s):
    return 5 if s == -1 else 8


def scan_bank(s, name):
    if name[0] == "o":
        return 7 if s < 0 else 0
    return 5 + int(name[2:]) % 2 if s < 0 else 2


MAXIMA = {}
for _which, _slot, _quarters, _heads in (("b", 0, 10 * NT, range(LAG, H)), ("o", 10, 5 * NT, range(LAG))):
    _tiles = [(_h, _i) for _h in _heads for _i in range(NT)]
    for _q in range(_quarters):
        MAXIMA[_slot + _q // NT, _q % NT] = [(_which, *_tile) for _tile in _tiles[
            _q * len(_tiles) // _quarters:(_q + 1) * len(_tiles) // _quarters]]
PARTS = {(2, 3): ("b", 1), (6, 2): ("b", 2), (10, 1): ("b", 3), (14, 0): ("o", 0)}
ROWS = {(3, 2): ("b", 1), (6, 3): ("b", 2), (10, 3): ("b", 3), (14, 3): ("o", 0)}


def number_uses():
    uses, signals, at = {}, {}, {}

    def use(name, batch, bank):
        if batch is None:
            return
        uses[bank] = uses.get(bank, 0) + 1
        if name not in ("o0", "o1"):
            signals[bank] = signals.get(bank, 0) + 1
        at[name, batch] = (bank, uses[bank], signals.get(bank, 0))

    for s in STEPS:
        stage = dict(zip("robfe", stages(s)))
        r = stage["r"]
        for n in range(H):
            for i in range(NT):
                slot = n - scan_slot(s)
                if 0 <= slot < DV // 2 and i % 2 == 0:
                    name = f"vb{2 * slot + i // 2}"
                    use(name, stage["r"], scan_bank(s, name))
                if (slot, i) in ((1, 1), (5, 1)):
                    use(f"o{slot // 4}", stage["r"], scan_bank(s, "o"))
                if r is not None and n == gate_slot(r) and i % 2 == 1:
                    use(f"gz{i // 2}", r, 1)
                if (n, i) in SIDE_USES:
                    name, which, bank = SIDE_USES[n, i]
                    use(name, stage[which], bank)
                for which, h, tile in MAXIMA.get((n, i), []):
                    use(f"m{h}.{tile}", stage[which], 3 + tile % 2)
                if (n, i) in ROWS:
                    which, g = ROWS[n, i]
                    use(f"mr{g}", stage[which], 3)
                use(f"s{n}.{i}", stage["b"], 5 + i % 2)
                if n % 4 == 1 and i == 0:
                    use(f"pv{n // 4}", stage["b"], 7)
    return at


USES = number_uses()
BANK = {name: use[0] for (name, _), use in USES.items()}

FIRST = 1


def count(per, b, n):
    return b * per + (n + FIRST)


def build(nc, t):
    ctx = ExitStack()
    with ctx:
        def sb(name, shape, dt=F32):
            return ctx.enter_context(nc.sbuf_tensor(name, shape, dt))

        counting = []

        def sem(name):
            counting.append(ctx.enter_context(nc.semaphore(name)))
            return counting[-1]

        banks = [ctx.enter_context(nc.psum_tensor(f"bank{i}", [P, 512], F32)) for i in range(8)]
        full = [sem(f"bank{i}_full") for i in range(8)]
        free = [sem(f"bank{i}_free") for i in range(8)]

        wq = sb("wq", [P, ND, P])
        wk = sb("wk", [P, ND, P])
        wg1 = sb("wg1", [P, ND, 16])
        wg2 = sb("wg2", [16, P])
        wv = sb("wv", [P, ND, D])
        wg = sb("wg", [P, ND, D])
        bg = sb("bg", [P, ND])
        wo = sb("wo", [P, ND, D])
        xwq = sb("xwq", [P, ND, D])
        xwk = sb("xwk", [P, ND, D])
        xwv = sb("xwv", [P, ND, D])
        xwo = sb("xwo", [P, NG, D])
        xbo = sb("xbo", [P, D])
        fwr = sb("fwr", [P, ND, D])
        fwk = sb("fwk", [P, ND, D])
        fwv = sb("fwv", [P, ND, D])
        mur = sb("mur", [P, ND])
        muk = sb("muk", [P, ND])
        hsel = sb("hsel", [P, 2, 32])
        vsel = sb("vsel", [3 * H, P], BF16)
        mavg = sb("mavg", [P, P])
        ident = sb("ident", [P, P])
        identb = sb("identb", [P, P], BF16)
        vsel32 = sb("vsel32", [3 * H, P])
        eps = sb("eps", [P, 1])
        one = sb("one", [P, 1])
        mhalf = sb("mhalf", [P, NT])
        eps4 = sb("eps4", [P, NT])
        zero = sb("zero", [P, 16])
        xT = sb("xT", [P, ND, S])
        xtok = sb("xtok", [P, NT, D])
        qT = sb("qT", [P, S])
        kT = sb("kT", [P, S])
        kg1 = sb("kg1", [16, S])
        VB = sb("VB", [3 * H, DV, S], BF16)
        kz = sb("kz", [P, 3, S])
        ab = sb("ab", [P, 3, S])
        U = sb("U", [P, 2, S])
        St = sb("St", [P, 2, S])
        Pq = sb("Pq", [P, 2, S])
        oS = sb("oS", [P, ND, S])
        sq = U
        rsd = ab[:, 1, :]
        x1 = sb("x1", [P, NT, D])
        x1b = sb("x1b", [P, 2, NT, D])
        x1T = sb("x1T", [P, ND, S])
        full32 = sb("full32", [P, ND, S])
        parts = sb("parts", [P, 3, ND, S], BF16)
        cT = sb("cT", [P, ND, S])
        KS = sb("KS", [NR, H, S], BF16)
        QS = sb("QS", [NR, H, S], BF16)
        Vs = sb("Vs", [P, NT, H, 32])
        MX = sb("MX", [P, H * NT])
        MR = sb("MR", [P, 2, 16])
        MP = sb("MP", [P, 8, 16], BF16)
        mrow = sb("mrow", [48, P], BF16)
        PT = sb("PT", [P, 2, NT, S])
        den = sb("den", [P, S])
        OT = sb("OT", [P, NG, S])
        x2 = sb("x2", [P, NT, D])
        x2T = sb("x2T", [P, ND, S + 1])
        xr = sb("xr", [P, ND, S])
        xk = sb("xk", [P, ND, S])
        ka = sb("ka", [P, ND, S])
        rl = sb("rl", [P, NT, D])
        ra = xr[:, :, :].rearrange("p a (t n) -> p (a t) n", n=D)
        y3 = rl
        st = [sb(f"st{n}", [P, NT, 6]) for n in range(3)]
        mv = [sb(f"mv{n}", [P, NT, 2]) for n in range(3)]
        rs = [sb(f"rs{n}", [P, NT]) for n in range(3)]

        w_in = ctx.enter_context(nc.semaphore("w_in"))
        w2_in = ctx.enter_context(nc.semaphore("w2_in"))
        cst = ctx.enter_context(nc.semaphore("cst"))
        ks_set = ctx.enter_context(nc.semaphore("ks_set"))
        xT_in = sem("xT_in"); xt_in = sem("xt_in"); cT_in = sem("cT_in")
        v_hi = sem("v_hi"); v_r1 = sem("v_r1"); v_mid = sem("v_mid"); v_lo = sem("v_lo")
        v_in = sem("v_in")
        kz_abs = sem("kz_abs"); kz_exp = sem("kz_exp"); kz_ln = sem("kz_ln")
        kz_ls = sem("kz_ls"); decay = sem("decay")
        z_abs = sem("z_abs"); z_exp = sem("z_exp"); z_ln = sem("z_ln"); z_ls = sem("z_ls"); z_sig = sem("z_sig")
        gate_z = sem("gate_z")
        s_done = sem("s_done"); p_done = sem("p_done"); r_done = sem("r_done")
        o_sq = sem("o_sq"); o_rs = sem("o_rs"); o_gate = sem("o_gate"); gated = sem("gated")
        st_done = [sem(f"st{n}_done") for n in range(3)]
        mv_done = [sem(f"mv{n}_done") for n in range(3)]
        ve_done = [sem(f"ve{n}_done") for n in range(3)]
        rs_done = [sem(f"rs{n}_done") for n in range(3)]
        x1_done = sem("x1_done"); x1b_done = sem("x1b_done")
        K_hi = sem("K_hi"); K_r1 = sem("K_r1"); K_mid = sem("K_mid"); K_lo = sem("K_lo"); K_out = sem("K_out")
        Q_hi = sem("Q_hi"); Q_r1 = sem("Q_r1"); Q_mid = sem("Q_mid"); Q_lo = sem("Q_lo"); Q_out = sem("Q_out")
        K_in = [sem(f"K_in{g}") for g in range(NG)]
        Q_in = [sem(f"Q_in{g}") for g in range(NG)]
        m_step = sem("m_step"); m_parts = sem("m_parts"); m_in = sem("m_in")
        pv_done = sem("pv_done"); d_sh = sem("d_sh"); d_ln = sem("d_ln"); d_inv = sem("d_inv"); normal = sem("normal")
        x2_done = sem("x2_done"); mix_p = sem("mix_p"); mix_done = sem("mix_done")
        r_abs = sem("r_abs"); r_exp = sem("r_exp"); r_ln = sem("r_ln"); r_ls = sem("r_ls"); r_sig = sem("r_sig")
        ka2 = sem("ka2"); f_mul = sem("f_mul"); x3_done = sem("x3_done"); o_out = sem("o_out")

        loads = [(wv, "wv"), (wg1, "wg1"), (wg2, "wg2"), (vsel32, "vsel"), (wq, "wq"), (wk, "wk"), (wg, "wg"),
                 (bg, "bg"), (ident, "ident"), (mur, "mur"), (muk, "muk"), (hsel, "hsel"), (mavg, "mavg")]
        loads2 = [(xwk, "xwk"), (wo, "wo"), (xwq, "xwq"), (xwv, "xwv"), (xwo, "xwo"),
                  (fwr, "fwr"), (fwk, "fwk"), (fwv, "fwv")]
        W_ALL = 16 * len(loads)
        W2_ALL = 16 * (len(loads2) + 1)
        CST = 9
        out_v = t["out"].rearrange("b (t p) d -> b p t d", p=P)
        xtok_v = t["x"].rearrange("b (t p) d -> b p t d", p=P)


        def full_of(name, b):
            bank, _, signal = USES.get((name, b), (0, 0, 0))
            return full[bank], signal + FIRST

        def free_for(name, b):
            bank, use, _ = USES[name, b]
            return free[bank], use - 1 + FIRST

        def read(name, b):
            bank, use, _ = USES[name, b]
            return free[bank], use + FIRST

        def bank_of(name, b):
            return BANK[name] if b is None else USES[name, b][0]

        def filled(name, b=None):
            return full[bank_of(name, b)]

        def emptied(name, b=None):
            return free[bank_of(name, b)]

        def bank(name, b=None):
            return banks[bank_of(name, b)]

        def tokens(name):
            return bank(name)[:, :].rearrange("p (t n) -> p t n", t=2)

        block = ctx.enter_context(nc.Block())

        @block.sync
        def _(sp):
            sp.dma_start(xT[:, :, :], t["xT"][0]).then_inc(xT_in, 16)
            for dst, name in loads:
                sp.dma_start(dst[tuple(slice(None) for _ in dst.shape)], t[name]).then_inc(w_in, 16)
            for s in counting:
                sp.sem_inc(s, FIRST)
            sp.dma_start(cT[:, :, :], t["cT"][0]).then_inc(cT_in, 16)
            for dst, name in loads2:
                sp.dma_start(dst[tuple(slice(None) for _ in dst.shape)], t[name]).then_inc(w2_in, 16)
            sp.dma_start(xbo[:, :], t["xbo"][None, :].broadcast_to([P, D])).then_inc(w2_in, 16)
            sp.dma_start(xtok[:, :, :], xtok_v[0]).then_inc(xt_in, 16)

            def keys_in(b, g):
                sp.wait_ge(ks_set, 3)
                sp.wait_ge(K_out, count(48, b, 48))
                sp.wait_ge(*full_of(f"s{4 * g + 3}.2", b - 1))
                sp.wait_ge(*full_of(f"s{4 * g + 3}.3", b - 1))
                for s, part in enumerate(SLOTS_K):
                    heads = t["k_parts"][b, part, g // 2].rearrange("(h d) n -> d h n", d=HD)
                    sp.dma_start(KS[HD * s:HD * s + HD, 4 * g:4 * g + 4, :],
                                 heads[:, 4 * (g % 2):4 * (g % 2) + 4, :]).then_inc(K_in[g], 16)

            def queries_in(b, g):
                sp.wait_ge(Q_out, count(48, b, 48))
                sp.wait_ge(*full_of(f"s{4 * g + 3}.2", b - 1))
                sp.wait_ge(*full_of(f"s{4 * g + 3}.3", b - 1))
                for s, part in enumerate(SLOTS_Q):
                    heads = t["q_parts"][b, part, g // 2].rearrange("(h d) n -> d h n", d=HD)
                    sp.dma_start(QS[HD * s:HD * s + HD, 4 * g:4 * g + 4, :],
                                 heads[:, 4 * (g % 2):4 * (g % 2) + 4, :]).then_inc(Q_in[g], 16)

            for s in STEPS:
                r, o, b, f, e = stages(s)
                if b is not None:
                    keys_in(b, NG - 1)
                    queries_in(b, NG - 1)
                if o is not None and b is not None:
                    sp.wait_ge(*full_of("V1", b))
                    sp.dma_start(cT[:, :, :], t["cT"][o]).then_inc(cT_in, 16)
                if e is not None:
                    sp.wait_ge(x3_done, count(NT, e, NT))
                    sp.dma_start(out_v[e], y3[:, :, :]).then_inc(o_out, 16)
                if r is not None:
                    sp.wait_ge(*full_of(f"vb{DV - 1}", r - 1))
                    sp.wait_ge(*full_of(f"vb{DV - 2}", r - 1))
                    for p, part in enumerate((v_hi, v_mid, v_lo)):
                        sp.wait_ge(part, count(1, r, 1))
                        for m in range(ND):
                            sp.dma_start(VB[H * p + 8 * m:H * p + 8 * m + 8, :, :], parts[:, p, m, :]).then_inc(v_in, 16)
                if o is not None:
                    for p, part in enumerate((K_hi, K_mid, K_lo)):
                        sp.wait_ge(part, count(1, o, 1))
                        sp.dma_start(t["k_parts"][o, p].rearrange("t p n -> p t n"), parts[:, p, :, :]).then_inc(K_out, 16)
                    keys_in(o, 0)
                    if o + 1 < B:
                        sp.wait_ge(x1_done, count(NT, o, NT))
                        sp.dma_start(xtok[:, :, :], xtok_v[o + 1]).then_inc(xt_in, 16)
                if o is not None:
                    keys_in(o, 1)
                    for p, part in enumerate((Q_hi, Q_mid, Q_lo)):
                        sp.wait_ge(part, count(1, o, 1))
                        sp.dma_start(t["q_parts"][o, p].rearrange("t p n -> p t n"), parts[:, p, :, :]).then_inc(Q_out, 16)
                    queries_in(o, 0)
                    queries_in(o, 1)
                if r is not None and r + 1 < B:
                    sp.wait_ge(*full_of("gz1", r))
                    sp.dma_start(xT[:, :, :], t["xT"][r + 1]).then_inc(xT_in, 16)
                if o is not None:
                    keys_in(o, 2)
                    queries_in(o, 2)
            sp.wait_ge(o_out, 16 * B + FIRST)
            sp.wait_ge(K_out, 48 * B + FIRST)
            sp.wait_ge(Q_out, 48 * B + FIRST)

        @block.tensor
        def _(pe):
            pe.wait_ge(w_in, W_ALL)
            pe.wait_ge(cst, CST)

            def project(out, w_of, x_of):
                for k in range(ND):
                    ins = pe.matmul(out, w_of(k), x_of(k), start=(k == 0), stop=(k == ND - 1))
                return ins

            def by_feature(name, b, w, m, x):
                pe.wait_ge(*free_for(name, b))
                project(bank(name)[:, :], lambda k: w[:, k, m * P:(m + 1) * P], lambda k: x[:, k, :]).then_inc(filled(name), 1)

            def by_token(name, b, x, w, m, tiles=ND):
                pe.wait_ge(*free_for(name, b))
                for half in range(2):
                    tt = 2 * m + half
                    for k in range(tiles):
                        ins = pe.matmul(bank(name)[:, half * D:(half + 1) * D], x[:, k, tt * P:(tt + 1) * P],
                                        w[:, k, :], start=(k == 0), stop=(k == tiles - 1))
                ins.then_inc(filled(name), 1)

            def turn(name, b, x, m):
                pe.wait_ge(*free_for(name, b))
                for tt in range(NT):
                    ins = pe.transpose(bank(name)[:, tt * P:(tt + 1) * P], x[:, tt, m * P:(m + 1) * P], ident[:, :])
                ins.then_inc(filled(name), 1)

            def broadcast_value(a, e):
                if e == 0:
                    pe.wait_ge(v_in, count(96, a, 96))
                pe.wait_ge(*free_for(f"vb{e}", a))
                pe.matmul(bank(f"vb{e}", a)[:, :], vsel[:, :], VB[:, e, :], start=True, stop=True).then_inc(filled(f"vb{e}", a), 1)

            def reduce_step(a, e):
                g, j, i = e // 8, (e % 8) // 2, e % 2
                pe.wait_ge(p_done, count(DV, a, e + 1))
                if e % 8 == 0:
                    pe.wait_ge(*free_for(f"o{g}", a))
                pe.matmul(bank(f"o{g}", a)[32 * j:32 * j + 32, :], hsel[:, i, :], Pq[:, e % 2, :],
                          start=(i == 0), stop=(i == 1)).then_inc(r_done, 1)

            def max_rows(b, g):
                pe.wait_ge(m_parts, count(NG, b, g + 1))
                pe.wait_ge(*free_for(f"mr{g}", b))
                pe.transpose(bank(f"mr{g}")[:, 0:P // 2].bitcast(BF16),
                             MP[:, :, :].rearrange("p s n -> p (s n)"), identb[:, :]).then_inc(filled(f"mr{g}"), 1)

            def max_tile(b, h, i):
                if h % 4 == 0 and i == 0:
                    pe.wait_ge(K_in[h // 4], count(96, b, 96))
                    pe.wait_ge(Q_in[h // 4], count(96, b, 96))
                n = f"m{h}.{i}"
                pe.wait_ge(*free_for(n, b))
                pe.matmul(bank(n)[:, :], QS[0:NS, h, i * P:(i + 1) * P], KS[0:NS, h, :],
                          start=True, stop=True).then_inc(filled(n), 1)

            def score_tile(b, h, i):
                if i == 0 and h % 4 == 0:
                    pe.wait_ge(m_in, count(16 * NG, b, 16 * (h // 4 + 1)))
                n = f"s{h}.{i}"
                pe.wait_ge(*free_for(n, b))
                pe.matmul(bank(n)[:, :], KS[0:NR, h, i * P:(i + 1) * P], QS[0:NR, h, :],
                          start=True, stop=True).then_inc(filled(n), 1)

            def value_tile(b, h, i):
                g, j = h // 4, h % 4
                pe.wait_ge(*read(f"s{h}.{i}", b))
                if h == 0 and i == 0:
                    pe.wait_ge(*read("V0", b))
                    pe.wait_ge(*read("V1", b))
                if j == 0 and i == 0:
                    pe.wait_ge(*free_for(f"pv{g}", b))
                ins = pe.matmul(bank(f"pv{g}")[32 * j:32 * j + 32, :], Vs[:, i, h, :], PT[:, h % 2, i, :],
                                start=(i == 0), stop=(i == NT - 1))
                if i == NT - 1:
                    ins.then_inc(pv_done, 1)

            def projecting(r, at, slot):
                if at == (1, 0):
                    pe.wait_ge(xT_in, count(16, r, 16))
                    by_feature("gv0", r, wv, 0, xT)
                if at == (1, 1):
                    by_feature("gv1", r, wv, 1, xT)
                if at == (1, 3):
                    pe.wait_ge(*free_for("gg1", r))
                    project(bank("gg1")[0:16, :], lambda k: wg1[:, k, :], lambda k: xT[:, k, :]).then_inc(filled("gg1"), 1)
                if at == (2, 3):
                    pe.wait_ge(*read("gg1", r))
                    pe.wait_ge(*free_for("gg", r))
                    pe.matmul(bank("gg")[:, :], wg2[:, :], kg1[:, :], start=True, stop=True).then_inc(filled("gg"), 1)
                if at == (3, 0):
                    by_feature("gq", r, wq, 0, xT)
                if at == (3, 1):
                    by_feature("gk", r, wk, 0, xT)
                if at in ((gate_slot(r), 1), (gate_slot(r), 3)):
                    m = at[1] // 2
                    by_feature(f"gz{m}", r, wg, m, xT)
                i = at[1]
                if 0 <= slot < DV // 2 and i % 2 == 0:
                    broadcast_value(r, 2 * slot + i // 2)
                if 1 <= slot <= DV // 2 and i % 2 == 1:
                    reduce_step(r, 2 * (slot - 1) + i // 2)

            def gated_end(o, at, slot):
                if slot == DV // 2 and at in ((0, 0), (0, 1)):
                    reduce_step(o, DV - 2 + at[1])
                if at == (1, 2):
                    pe.wait_ge(*read("o0", o))
                    pe.wait_ge(*read("o1", o))
                    pe.wait_ge(*free_for("mean", o))
                    project(bank("mean")[:, :], lambda k: mavg[:, :], lambda k: oS[:, k, :]).then_inc(filled("mean"), 1)
                if at == (2, 2):
                    pe.wait_ge(o_sq, count(1, o, 1))
                    pe.wait_ge(*free_for("var", o))
                    project(bank("var")[:, :], lambda k: mavg[:, :], lambda k: sq[:, k, :]).then_inc(filled("var"), 1)
                if at == (3, 2):
                    pe.wait_ge(w2_in, W2_ALL)
                    pe.wait_ge(cT_in, count(16, o, 16))
                    by_feature("K0", o, xwk, 0, cT)
                if at == (3, 3):
                    by_feature("K1", o, xwk, 1, cT)
                if at == (4, 2):
                    pe.wait_ge(gated, count(1, o, 1))
                    by_token("gy0", o, oS, wo, 0)
                if at == (4, 3):
                    by_token("gy1", o, oS, wo, 1)
                if at == (6, 0):
                    pe.wait_ge(x1_done, count(NT, o, NT))
                    turn("gt0", o, x1, 0)
                if at == (6, 1):
                    turn("gt1", o, x1, 1)
                if at == (7, 0):
                    pe.wait_ge(*read("gt0", o))
                    pe.wait_ge(*read("gt1", o))
                    by_feature("Q0", o, xwq, 0, x1T)
                if at == (7, 1):
                    by_feature("Q1", o, xwq, 1, x1T)

            def feed_forward(f, at):
                if at == (2, 0):
                    pe.wait_ge(normal, count(NG, f, NG))
                    by_token("y0", f, OT, xwo, 0, NG)
                if at == (2, 1):
                    by_token("y1", f, OT, xwo, 1, NG)
                if at == (4, 0):
                    pe.wait_ge(x2_done, count(NT, f, NT))
                    turn("t0", f, x2, 0)
                if at == (4, 1):
                    turn("t1", f, x2, 1)
                if at == (5, 3):
                    pe.wait_ge(mix_done, count(2, f, 1))
                    by_token("r0", f, xr, fwr, 0)
                if at == (6, 2):
                    by_token("r1", f, xr, fwr, 1)
                if at == (8, 1):
                    pe.wait_ge(mix_done, count(2, f, 2))
                    by_feature("f0", f, fwk, 0, xk)
                if at == (8, 3):
                    by_feature("f1", f, fwk, 1, xk)
                if at == (11, 3):
                    pe.wait_ge(ka2, count(2, f, 2))
                    by_token("w0", f, ka, fwv, 0)
                if at == (12, 3):
                    by_token("w1", f, ka, fwv, 1)

            for s in STEPS:
                r, o, b, f, e = stages(s)
                stage = {"r": r, "o": o, "b": b, "f": f, "e": e}
                for n in range(H):
                    for i in range(NT):
                        if b is not None:
                            score_tile(b, n, i)
                        if r is not None:
                            projecting(r, (n, i), n - scan_slot(s))
                        if o is not None:
                            gated_end(o, (n, i), n + H - scan_slot(s - 1))
                        if f is not None:
                            feed_forward(f, (n, i))
                        if b is not None and n == 0 and i < 2:
                            by_token(f"V{i}", b, cT, xwv, i)
                        for which, h, tile in MAXIMA.get((n, i), []):
                            if stage[which] is not None:
                                max_tile(stage[which], h, tile)
                        if (n, i) in ROWS and stage[ROWS[n, i][0]] is not None:
                            max_rows(stage[ROWS[n, i][0]], ROWS[n, i][1])
                        if n >= 1 and b is not None:
                            value_tile(b, n - 1, i)
                        if n == 0 and f is not None:
                            value_tile(f, H - 1, i)

        @block.scalar
        def _(act):
            act.preload_act_table_set("natural_log_exp_and_others")
            act.wait_ge(w_in, W_ALL)
            act.wait_ge(cst, CST)

            def projecting(r, at, slot):
                if at in ((1, 2), (1, 3)):
                    m = at[1] - 2
                    act.wait_ge(*full_of(f"gv{m}", r))
                    if m == 0:
                        act.wait_ge(Q_lo, count(1, r - 2, 1) if r >= 2 else FIRST)
                    act.activation(full32[:, m, :], bank(f"gv{m}")[:, :], ACT.Copy).then_inc(emptied(f"gv{m}"), 1)
                if at == (1, 3):
                    act.wait_ge(*read("gv0", r))
                    act.wait_ge(*read("gv1", r))
                    act.wait_ge(Q_out, count(48, r - 2, 48) if r >= 2 else FIRST)
                    act.activation(parts[:, 0, :, :], full32[:, :, :], ACT.Copy).then_inc(v_hi, 1)
                if at == (2, 0):
                    act.wait_ge(*full_of("gg1", r))
                    act.activation(kg1[:, :], bank("gg1")[0:16, :], ACT.Copy).then_inc(emptied("gg1"), 1)
                if at == (2, 3):
                    act.wait_ge(v_r1, count(1, r, 1))
                    act.activation(parts[:, 1, :, :], full32[:, :, :], ACT.Copy).then_inc(v_mid, 1)
                if at == (3, 1):
                    act.wait_ge(*full_of("gg", r))
                    act.activation(kz[:, 0, :], bank("gg")[:, :], ACT.Copy).then_inc(emptied("gg"), 1)
                if at == (3, 2):
                    act.wait_ge(*full_of("gq", r))
                    act.wait_ge(p_done, count(DV, r, 0))
                    act.activation(qT[:, :], bank("gq")[:, :], ACT.Copy).then_inc(emptied("gq"), 1)
                if at == (3, 3):
                    act.wait_ge(*full_of("gk", r))
                    act.wait_ge(s_done, count(DV, r, 0))
                    act.activation(kT[:, :], bank("gk")[:, :], ACT.Copy, scale=float(DK) ** -0.5).then_inc(emptied("gk"), 1)
                if at == (3, 3):
                    act.wait_ge(*read("gg", r))
                    act.wait_ge(s_done, count(DV, r, 0))
                    act.activation(ab[:, 0, :], kz[:, 0, :], ACT.Abs).then_inc(kz_abs, 1)
                if at == (4, 0):
                    act.wait_ge(kz_abs, count(1, r, 1))
                    act.activation(ab[:, 0, :], ab[:, 0, :], ACT.Exp, scale=-1.0).then_inc(kz_exp, 1)
                if at == (4, 1):
                    act.wait_ge(kz_exp, count(1, r, 1))
                    act.activation(ab[:, 0, :], ab[:, 0, :], ACT.Ln, bias=one[:, :]).then_inc(kz_ln, 1)
                if at == (5, 1):
                    act.wait_ge(kz_ls, count(1, r, 1))
                    act.activation(ab[:, 0, :], ab[:, 0, :], ACT.Exp, scale=1.0 / 16.0).then_inc(decay, 1)
                if at in ((gate_slot(r), 2), (gate_slot(r) + 1, 1)):
                    m = at[0] - gate_slot(r)
                    act.wait_ge(*full_of(f"gz{m}", r))
                    act.wait_ge(o_gate, count(1, r, 0))
                    act.activation(kz[:, 1 + m, :], bank(f"gz{m}")[:, :], ACT.Identity,
                                   bias=bg[:, m:m + 1]).then_inc(emptied(f"gz{m}"), 1)
                if at == (11, 2):
                    act.wait_ge(*read("gz0", r))
                    act.wait_ge(*read("gz1", r))
                    act.wait_ge(gated, count(1, r, 0))
                    act.activation(ab[:, 1:3, :], kz[:, 1:3, :], ACT.Abs).then_inc(z_abs, 1)
                if at == (12, 0):
                    act.wait_ge(z_abs, count(1, r, 1))
                    act.activation(ab[:, 1:3, :], ab[:, 1:3, :], ACT.Exp, scale=-1.0).then_inc(z_exp, 1)
                if at == (12, 3):
                    act.wait_ge(z_exp, count(1, r, 1))
                    act.activation(ab[:, 1:3, :], ab[:, 1:3, :], ACT.Ln, bias=one[:, :]).then_inc(z_ln, 1)
                if (slot, at[1]) == (5, 0):
                    act.wait_ge(r_done, count(DV, r, 8))
                    act.wait_ge(*full_of("gy1", r - 1))
                    act.activation(oS[:, 0, :], bank("o0", r)[:, :], ACT.Copy).then_inc(emptied("o0", r), 1)

            def gated_end(o, at):
                if at == (0, 3):
                    act.wait_ge(z_ls, count(1, o, 1))
                    act.activation(ab[:, 1:3, :], ab[:, 1:3, :], ACT.Exp).then_inc(z_sig, 1)
                if at == (0, 2):
                    act.wait_ge(r_done, count(DV, o, DV))
                    act.activation(oS[:, 1, :], bank("o1", o)[:, :], ACT.Copy).then_inc(emptied("o1", o), 1)
                if at == (2, 1):
                    act.wait_ge(*read("mean", o))
                    act.activation(sq[:, :, :], oS[:, :, :], ACT.Square).then_inc(o_sq, 1)
                if at == (3, 0):
                    act.wait_ge(*full_of("var", o))
                    act.wait_ge(gate_z, count(1, o, 1))
                    act.activation(rsd, bank("var")[:, :], ACT.Ln, bias=eps[:, :]).then_inc(emptied("var"), 1)
                    act.wait_ge(*read("var", o))
                    act.activation(rsd, rsd, ACT.Exp, scale=-0.5).then_inc(o_rs, 1)
                if at == (4, 0):
                    for m in range(ND):
                        act.wait_ge(*full_of(f"K{m}", o))
                        act.wait_ge(v_lo, count(1, min(o + 1, B - 1), 1))
                        act.activation(full32[:, m, :], bank(f"K{m}")[:, :], ACT.Copy).then_inc(emptied(f"K{m}"), 1)
                    act.wait_ge(*read("K0", o))
                    act.wait_ge(*read("K1", o))
                    act.wait_ge(v_in, count(96, min(o + 1, B - 1), 96))
                    act.wait_ge(Q_out, count(48, o, 0))
                    act.activation(parts[:, 0, :, :], full32[:, :, :], ACT.Copy).then_inc(K_hi, 1)
                if at == (5, 0):
                    act.wait_ge(K_r1, count(1, o, 1))
                    act.activation(parts[:, 1, :, :], full32[:, :, :], ACT.Copy).then_inc(K_mid, 1)
                if at == (6, 2):
                    for m in range(ND):
                        act.wait_ge(*full_of(f"gt{m}", o))
                        act.wait_ge(*full_of("Q1", o - 1))
                        act.activation(x1T[:, m, :], bank(f"gt{m}")[:, :], ACT.Copy).then_inc(emptied(f"gt{m}"), 1)
                if at == (7, 2):
                    for m in range(ND):
                        act.wait_ge(*full_of(f"Q{m}", o))
                        act.wait_ge(K_lo, count(1, o, 1))
                        act.activation(full32[:, m, :], bank(f"Q{m}")[:, :], ACT.Copy,
                                       scale=float(HD) ** -0.5).then_inc(emptied(f"Q{m}"), 1)
                    act.wait_ge(*read("Q0", o))
                    act.wait_ge(*read("Q1", o))
                    act.wait_ge(K_out, count(48, o, 48))
                    act.activation(parts[:, 0, :, :], full32[:, :, :], ACT.Copy).then_inc(Q_hi, 1)
                if at == (8, 1):
                    act.wait_ge(Q_r1, count(1, o, 1))
                    act.activation(parts[:, 1, :, :], full32[:, :, :], ACT.Copy).then_inc(Q_mid, 1)

            def feed_forward(f, at):
                if at == (4, 2):
                    for m in range(ND):
                        act.wait_ge(*full_of(f"t{m}", f))
                        act.wait_ge(mix_done, count(2, f, 0))
                        act.activation(x2T[:, m, 1:S + 1], bank(f"t{m}")[:, :], ACT.Copy).then_inc(emptied(f"t{m}"), 1)
                if at in ((6, 1), (7, 0)):
                    m = at[0] - 6
                    act.wait_ge(*full_of(f"r{m}", f))
                    act.wait_ge(o_out, count(16, f, 0))
                    act.activation(rl[:, 2 * m:2 * m + 2, :], tokens(f"r{m}"), ACT.Copy).then_inc(emptied(f"r{m}"), 1)
                if at == (8, 1):
                    act.wait_ge(*read("r1", f))
                    act.wait_ge(x3_done, count(NT, f, 0))
                    act.activation(ra[:, :, :], rl[:, :, :], ACT.Abs).then_inc(r_abs, 1)
                if at == (9, 0):
                    act.wait_ge(r_abs, count(1, f, 1))
                    act.activation(ra[:, :, :], ra[:, :, :], ACT.Exp, scale=-1.0).then_inc(r_exp, 1)
                if at == (9, 2):
                    act.wait_ge(r_exp, count(1, f, 1))
                    act.activation(ra[:, :, :], ra[:, :, :], ACT.Ln, bias=one[:, :]).then_inc(r_ln, 1)
                if at in ((8, 3), (9, 1)):
                    m = at[0] - 8
                    act.wait_ge(*full_of(f"f{m}", f))
                    act.wait_ge(*full_of("w1", f - 1))
                    act.activation(ka[:, m, :], bank(f"f{m}")[:, :], ACT.Relu).then_inc(emptied(f"f{m}"), 1)
                    act.wait_ge(*read(f"f{m}", f))
                    act.activation(ka[:, m, :], ka[:, m, :], ACT.Square).then_inc(ka2, 1)
                if at == (10, 3):
                    act.wait_ge(r_ls, count(1, f, 1))
                    act.activation(ra[:, :, :], ra[:, :, :], ACT.Exp).then_inc(r_sig, 1)

            def max_rows(b, g):
                act.wait_ge(*full_of(f"mr{g}", b))
                act.wait_ge(m_in, count(16 * NG, b, 16 * g))
                act.activation(mrow[:, :], bank(f"mr{g}")[0:48, 0:P // 2].bitcast(BF16), ACT.Copy).then_inc(emptied(f"mr{g}"), 1)
                act.wait_ge(*read(f"mr{g}", b))
                act.dma_start(QS[NS:NR, 4 * g:4 * g + 4, :], mrow[:, :]).then_inc(m_in, 16)

            def exp_tile(b, h, i):
                n = f"s{h}.{i}"
                act.wait_ge(*full_of(n, b))
                if i == 0:
                    act.wait_ge(pv_done, FIRST + max(H * b + h - 1, 0))
                act.activation(PT[:, h % 2, i, :], bank(n)[:, :], ACT.Exp).then_inc(emptied(n), 1)

            def unload(b, g):
                act.wait_ge(pv_done, count(H, b, 4 * (g + 1)))
                act.wait_ge(*full_of("y1", b - 1))
                act.activation(OT[:, g, :], bank(f"pv{g}")[:, :], ACT.Copy).then_inc(emptied(f"pv{g}"), 1)

            def invert(b, g):
                act.wait_ge(d_sh, count(NG, b, g + 1))
                act.activation(den[:, :], den[:, :], ACT.Ln).then_inc(d_ln, 1)
                act.wait_ge(d_ln, count(NG, b, g + 1))
                act.activation(den[:, :], den[:, :], ACT.Exp, scale=-1.0).then_inc(d_inv, 1)

            for s in STEPS:
                r, o, b, f, e = stages(s)
                stage = {"r": r, "o": o, "b": b, "f": f, "e": e}
                for n in range(H):
                    group = ((f, NG - 1) if n == 1 else (b, n // 4 - 1)) if n % 4 == 1 else (None, None)
                    for i in range(NT):
                        if i == 0 and group[0] is not None:
                            unload(*group)
                        if r is not None:
                            projecting(r, (n, i), n - scan_slot(s))
                        if f is not None:
                            feed_forward(f, (n, i))
                        if o is not None:
                            gated_end(o, (n, i))
                        if b is not None:
                            exp_tile(b, n, i)
                        if (n, i) in ROWS and stage[ROWS[n, i][0]] is not None:
                            max_rows(stage[ROWS[n, i][0]], ROWS[n, i][1])
                        if i == 2 and group[0] is not None:
                            invert(*group)
                        if n == 0 and i == 3 and b is not None:
                            for m in range(2):
                                act.wait_ge(*full_of(f"V{m}", b))
                                act.wait_ge(pv_done, count(H, b, 0))
                                act.activation(Vs[:, 2 * m:2 * m + 2, :, 0:HD],
                                               bank(f"V{m}")[:, :].rearrange("p (t h e) -> p t h e", t=2, e=HD),
                                               ACT.Copy).then_inc(emptied(f"V{m}"), 1)

        @block.vector
        def _(dve):
            dve.memset(eps[:, :], EPS).then_inc(cst, 1)
            dve.memset(eps4[:, :], EPS).then_inc(cst, 1)
            dve.memset(zero[:, :], 0.0).then_inc(cst, 1)
            dve.memset(MP[:, :, :], 0.0).then_inc(cst, 1)
            dve.memset(one[:, :], 1.0).then_inc(cst, 1)
            dve.memset(x2T[:, :, 0:1], 0.0).then_inc(cst, 1)
            dve.wait_ge(w_in, W_ALL)
            dve.tensor_copy(vsel[:, :], vsel32[:, :]).then_inc(cst, 1)
            dve.tensor_copy(identb[:, :], ident[:, :]).then_inc(cst, 1)
            dve.memset(Vs[:, :, :, HD:HD + 1], 1.0).then_inc(ks_set, 1)
            dve.memset(Vs[:, :, :, HD + 1:32], 0.0).then_inc(ks_set, 1)
            dve.memset(KS[NS:NR, :, :], -1.0).then_inc(ks_set, 1)
            dve.wait_ge(cst, CST)

            def first_rest(hi, r1, b):
                dve.wait_ge(hi, count(1, b, 1))
                dve.tensor_tensor(full32[:, :, :], full32[:, :, :], parts[:, 0, :, :], ALU.subtract).then_inc(r1, 1)

            def second_rest(mid, lo, b):
                dve.wait_ge(mid, count(1, b, 1))
                dve.tensor_tensor(parts[:, 2, :, :], full32[:, :, :], parts[:, 1, :, :], ALU.subtract).then_inc(lo, 1)

            def statistics(n, src, b):
                for tt in range(NT):
                    ins = dve.bn_stats(st[n][:, tt, :], src[:, tt, :])
                ins.then_inc(st_done[n], 1)
                dve.wait_ge(st_done[n], count(1, b, 1))
                for tt in range(NT):
                    ins = dve.bn_aggr(mv[n][:, tt, :], st[n][:, tt, :])
                ins.then_inc(mv_done[n], 1)

            def norm(n, src, dst, done, b):
                dve.wait_ge(rs_done[n], count(1, b, 1))
                for tt in range(NT):
                    dve.tensor_scalar(dst[:, tt, :], src[:, tt, :], mv[n][:, tt, 0:1], rs[n][:, tt:tt + 1],
                                      ALU.subtract, ALU.mult).then_inc(done, 1)

            def projecting(r, at, slot):
                if at == (1, 3):
                    first_rest(v_hi, v_r1, r)
                if at == (2, 2):
                    second_rest(v_mid, v_lo, r)
                if at == (4, 2):
                    dve.wait_ge(kz_ln, count(1, r, 1))
                    dve.scalar_tensor_tensor(ab[:, 0, :], kz[:, 0, :], 0.0, ab[:, 0, :], ALU.min, ALU.subtract)\
                       .then_inc(kz_ls, 1)
                i = at[1]
                if 0 <= slot < DV // 2:
                    e = 2 * slot + i // 2
                    if i % 2 == 0:
                        dve.wait_ge(*full_of(f"vb{e}", r))
                        if e == 0:
                            dve.wait_ge(*read("gk", r))
                        dve.tensor_tensor(U[:, e % 2, :], kT[:, :], bank(f"vb{e}", r)[:, :], ALU.mult).then_inc(emptied(f"vb{e}", r), 1)
                    else:
                        dve.wait_ge(*read(f"vb{e}", r))
                        if e == 1 or e == 0:
                            dve.wait_ge(decay, count(1, r, 1))
                        dve.wait_ge(p_done, count(DV, r, max(e - 1, 0)))
                        dve.tensor_tensor_scan(St[:, e % 2, :], ab[:, 0, :], U[:, e % 2, :], 0.0, ALU.mult, ALU.add)\
                           .then_inc(s_done, 1)

            def gated_end(o, at):
                if at == (4, 1):
                    first_rest(K_hi, K_r1, o)
                if at == (7, 3):
                    first_rest(Q_hi, Q_r1, o)
                if at == (8, 2):
                    second_rest(Q_mid, Q_lo, o)
                if at == (0, 1):
                    dve.wait_ge(z_ln, count(1, o, 1))
                    dve.scalar_tensor_tensor(ab[:, 1:3, :], kz[:, 1:3, :], 0.0, ab[:, 1:3, :], ALU.min, ALU.subtract)\
                       .then_inc(z_ls, 1)
                if at == (2, 0):
                    dve.wait_ge(*full_of("mean", o))
                    for g in range(ND):
                        ins = dve.tensor_tensor(oS[:, g, :], oS[:, g, :], bank("mean")[:, :], ALU.subtract)
                    ins.then_inc(emptied("mean"), 1)
                if at == (5, 0):
                    for m in range(2):
                        dve.wait_ge(*full_of(f"gy{m}", o))
                        if m == 0:
                            dve.wait_ge(xt_in, count(16, o, 16))
                        dve.tensor_tensor(xtok[:, 2 * m:2 * m + 2, :], tokens(f"gy{m}"),
                                          xtok[:, 2 * m:2 * m + 2, :], ALU.add).then_inc(emptied(f"gy{m}"), 1)
                    dve.wait_ge(*read("gy0", o))
                    dve.wait_ge(*read("gy1", o))
                    statistics(0, xtok, o)
                if at == (5, 2):
                    dve.wait_ge(x1b_done, count(1, o, 0))
                    dve.wait_ge(*full_of("gt1", o - 1))
                    norm(0, xtok, x1, x1_done, o)

            def feed_forward(f, at):
                xb = x1b[:, f % 2, :, :]
                if at == (2, 2):
                    for m in range(2):
                        dve.wait_ge(*full_of(f"y{m}", f))
                        if m == 0:
                            dve.wait_ge(x1b_done, count(1, f, 1))
                        dve.tensor_tensor(xb[:, 2 * m:2 * m + 2, :], tokens(f"y{m}"),
                                          xb[:, 2 * m:2 * m + 2, :], ALU.add).then_inc(emptied(f"y{m}"), 1)
                if at == (2, 3):
                    dve.wait_ge(*read("y0", f))
                    dve.wait_ge(*read("y1", f))
                    statistics(1, xb, f)
                if at == (3, 1):
                    dve.wait_ge(*full_of("t1", f - 1))
                    dve.wait_ge(x3_done, count(NT, f, 0))
                    norm(1, xb, x2, x2_done, f)
                if at == (4, 3):
                    dve.wait_ge(*read("t0", f))
                    dve.wait_ge(*read("t1", f))
                    dve.wait_ge(*full_of("f1", f - 1))
                    dve.tensor_tensor(xk[:, :, :], x2T[:, :, 1:S + 1], x2T[:, :, 0:S], ALU.subtract).then_inc(mix_p, 1)
                if at in ((5, 1), (6, 1)):
                    mu, dst = ((mur, xr), (muk, xk))[at[0] - 5]
                    dve.wait_ge(mix_p, count(1, f, 1))
                    dve.wait_ge(*full_of("r1", f - 1))
                    for m in range(ND):
                        ins = dve.scalar_tensor_tensor(dst[:, m, :], xk[:, m, :], mu[:, m:m + 1], x2T[:, m, 0:S],
                                                       ALU.mult, ALU.add)
                    ins.then_inc(mix_done, 1)
                if at == (10, 1):
                    dve.wait_ge(r_ln, count(1, f, 1))
                    dve.scalar_tensor_tensor(ra[:, :, :], rl[:, :, :], 0.0, ra[:, :, :], ALU.min, ALU.subtract)\
                       .then_inc(r_ls, 1)
                if at in ((12, 1), (13, 1)):
                    m = at[0] - 12
                    dve.wait_ge(r_sig, count(1, f, 1))
                    dve.wait_ge(*full_of(f"w{m}", f))
                    dve.tensor_tensor(ra[:, 2 * m:2 * m + 2, :], tokens(f"w{m}"),
                                      ra[:, 2 * m:2 * m + 2, :], ALU.mult).then_inc(emptied(f"w{m}"), 1)

            def last_norm(e, at):
                if at == (0, 2):
                    dve.wait_ge(*read("w1", e))
                    dve.tensor_tensor(ra[:, :, :], ra[:, :, :], x2[:, :, :], ALU.add).then_inc(f_mul, 1)
                if at == (0, 3):
                    dve.wait_ge(f_mul, count(1, e, 1))
                    statistics(2, ra, e)
                if at == (1, 2):
                    norm(2, ra, y3, x3_done, e)

            def max_tile(b, h, i):
                n = f"m{h}.{i}"
                dve.wait_ge(*full_of(n, b))
                if h % 4 == 0 and i == 0:
                    dve.wait_ge(m_parts, count(NG, b - 1, h // 4 + 1) if b else FIRST)
                dve.tensor_reduce(MX[:, NT * h + i:NT * h + i + 1], bank(n)[:, :], AX.X, ALU.max).then_inc(emptied(n), 1)

            def spread(b, g):
                dve.wait_ge(*read(f"pv{g}", b))
                dve.wait_ge(normal, count(NG, b, g))
                dve.stream_shuffle(den[:, :], OT[:, g, :], [HD] * 32).then_inc(d_sh, 1)

            def normalise(b, g):
                dve.wait_ge(d_inv, count(NG, b, g + 1))
                dve.tensor_tensor(OT[:, g, :], OT[:, g, :], den[:, :], ALU.mult).then_inc(normal, 1)

            for s in STEPS:
                r, o, b, f, e = stages(s)
                stage = {"r": r, "o": o, "b": b, "f": f, "e": e}
                for n in range(H):
                    group = ((f, NG - 1) if n == 1 else (b, n // 4 - 1)) if n % 4 == 1 else (None, None)
                    for i in range(NT):
                        if e is not None:
                            last_norm(e, (n, i))
                        if f is not None:
                            feed_forward(f, (n, i))
                        if o is not None:
                            gated_end(o, (n, i))
                        if r is not None:
                            projecting(r, (n, i), n - scan_slot(s))
                        for which, h, tile in MAXIMA.get((n, i), []):
                            if stage[which] is not None:
                                max_tile(stage[which], h, tile)
                        if group[0] is not None and i == 1:
                            spread(*group)
                        if group[0] is not None and i == 3:
                            normalise(*group)

        @block.gpsimd
        def _(pool):
            pool.memset(mhalf[:, :], -0.5).then_inc(cst, 1)
            pool.wait_ge(w_in, W_ALL)
            pool.wait_ge(cst, CST)

            def second_rest(mid, lo, b):
                pool.wait_ge(mid, count(1, b, 1))
                pool.tensor_tensor(parts[:, 2, :, :], full32[:, :, :], parts[:, 1, :, :], ALU.subtract).then_inc(lo, 1)

            def inverse_deviation(n, b):
                pool.wait_ge(mv_done[n], count(1, b, 1))
                pool.tensor_tensor(rs[n][:, :], mv[n][:, :, 1], eps4[:, :], ALU.add).then_inc(ve_done[n], 1)
                pool.wait_ge(ve_done[n], count(1, b, 1))
                pool.tensor_tensor(rs[n][:, :], rs[n][:, :], mhalf[:, :], ALU.pow).then_inc(rs_done[n], 1)

            def projecting(r, at, slot):
                i = at[1]
                if 0 <= slot < DV // 2 and i % 2 == 1:
                    e = 2 * slot + i // 2
                    pool.wait_ge(s_done, count(DV, r, e + 1))
                    if e == 0:
                        pool.wait_ge(*read("gq", r))
                    pool.wait_ge(r_done, count(DV, r, max(e - 1, 0)))
                    pool.tensor_tensor(Pq[:, e % 2, :], qT[:, :], St[:, e % 2, :], ALU.mult).then_inc(p_done, 1)

            def gated_end(o, at):
                if at == (1, 0):
                    pool.wait_ge(z_sig, count(1, o, 1))
                    pool.tensor_tensor(kz[:, 1:3, :], kz[:, 1:3, :], ab[:, 1:3, :], ALU.mult).then_inc(gate_z, 1)
                if at == (2, 1):
                    pool.wait_ge(o_sq, count(1, o, 1))
                    pool.wait_ge(gate_z, count(1, o, 1))
                    pool.tensor_tensor(oS[:, :, :], oS[:, :, :], kz[:, 1:3, :], ALU.mult).then_inc(o_gate, 1)
                if at == (3, 1):
                    pool.wait_ge(o_rs, count(1, o, 1))
                    pool.wait_ge(o_gate, count(1, o, 1))
                    pool.tensor_tensor(oS[:, :, :], oS[:, :, :], rsd.unsqueeze(1).broadcast_to([P, ND, S]),
                                       ALU.mult).then_inc(gated, 1)
                if at == (5, 0):
                    second_rest(K_mid, K_lo, o)
                if at == (5, 1):
                    inverse_deviation(0, o)
                if at == (6, 3):
                    pool.wait_ge(w2_in, W2_ALL)
                    pool.wait_ge(x1_done, count(NT, o, NT))
                    pool.wait_ge(x2_done, count(NT, o - 1, 0) if o else FIRST)
                    pool.tensor_tensor(x1b[:, o % 2, :, :], x1[:, :, :], xbo[:, :].unsqueeze(1).broadcast_to([P, NT, D]),
                                       ALU.add).then_inc(x1b_done, 1)

            def feed_forward(f, at):
                if at == (2, 3):
                    inverse_deviation(1, f)
            def max_parts(b, g):
                pool.wait_ge(*read(f"m{4 * g + 3}.{NT - 2}", b))
                pool.wait_ge(*read(f"m{4 * g + 3}.{NT - 1}", b))
                pool.wait_ge(*full_of(f"mr{(g - 1) % NG}", b if g else b - 1))
                m = MX[:, 16 * g:16 * g + 16]
                ops = [lambda: pool.tensor_tensor(MP[:, 0, :], m, zero[:, :], ALU.add),
                       lambda: pool.tensor_tensor(MR[:, 0, :], m, MP[:, 0, :], ALU.subtract),
                       lambda: pool.tensor_tensor(MP[:, 1, :], MR[:, 0, :], zero[:, :], ALU.add)]
                for k, op in enumerate(ops):
                    op().then_inc(m_step, 1)
                    pool.wait_ge(m_step, count(3 * NG, b, 3 * g + k + 1))
                pool.tensor_tensor(MP[:, 2, :], MR[:, 0, :], MP[:, 1, :], ALU.subtract).then_inc(m_parts, 1)

            for s in STEPS:
                r, o, b, f, e = stages(s)
                stage = {"r": r, "o": o, "b": b, "f": f, "e": e}
                for n in range(H):
                    for i in range(NT):
                        if (n, i) in PARTS and stage[PARTS[n, i][0]] is not None:
                            max_parts(stage[PARTS[n, i][0]], PARTS[n, i][1])
                        if e is not None and (n, i) == (1, 0):
                            inverse_deviation(2, e)
                        if f is not None:
                            feed_forward(f, (n, i))
                        if o is not None:
                            gated_end(o, (n, i))
                        if r is not None:
                            projecting(r, (n, i), n - scan_slot(s))


def layouts(i):
    import numpy as np

    def rows(w):
        return np.ascontiguousarray(w.reshape(-1, P, w.shape[1]).transpose(1, 0, 2))

    def by_feature(x):
        return np.ascontiguousarray(x.transpose(0, 2, 1).reshape(B, ND, P, S).transpose(0, 2, 1, 3))

    eh = np.arange(D).reshape(H, DV).T.reshape(-1)
    xwo = np.zeros((NG, 4, 32, D), np.float32)
    xwo[:, :, :HD] = i["L0_xattn_W_o"].reshape(NG, 4, HD, D)
    hsel = np.zeros((P, 2, 32), np.float32)
    vsel = np.zeros((3 * H, P), np.float32)
    for r in range(P):
        for s in range(2):
            hsel[r, s, 16 * s + r // DK] = 1
        for s in range(3):
            vsel[H * s + r // DK, r] = 1
    r = np.arange(P)
    mavg = ((r[:, None] % H) == (r[None, :] % H)).astype(np.float32) / DV
    return {
        "x": i["x"], "xT": by_feature(i["x"]), "cT": by_feature(i["ctx_1024"]),
        "wq": rows(i["L0_attn_Wq"]), "wk": rows(i["L0_attn_Wk"]), "wg1": rows(i["L0_attn_Wg1"]),
        "wg2": i["L0_attn_Wg2"], "wv": rows(i["L0_attn_Wv"]),
        "wg": rows(i["L0_attn_Wg"][:, eh]), "bg": np.ascontiguousarray(i["L0_attn_bg"][eh].reshape(ND, P).T),
        "wo": rows(i["L0_attn_Wo"][eh]),
        "xwq": rows(i["L0_xattn_W_q"]), "xwk": rows(i["L0_xattn_W_k"]), "xwv": rows(i["L0_xattn_W_v"]),
        "xwo": np.ascontiguousarray(xwo.reshape(NG, P, D).transpose(1, 0, 2)), "xbo": i["L0_xattn_b_o"],
        "fwr": rows(i["L0_ffn_W_r"].T), "fwk": rows(i["L0_ffn_W_k"].T), "fwv": rows(i["L0_ffn_W_v"].T),
        "mur": np.ascontiguousarray(i["L0_ffn_mu_r"].reshape(ND, P).T),
        "muk": np.ascontiguousarray(i["L0_ffn_mu_k"].reshape(ND, P).T),
        "hsel": hsel, "vsel": vsel, "mavg": mavg,
        "ident": np.eye(P, dtype=np.float32),
    }


def kernel(**inputs):
    import numpy as np
    import concourse.bacc as bacc
    from concourse.bass_utils import run_bass_kernel_spmd

    nc = bacc.Bacc("TRN2", target_bir_lowering=False, num_devices=1)
    arrays, t = {}, {}
    for name, a in layouts({k: np.asarray(v) for k, v in inputs.items()}).items():
        arrays[f"in_{name}"] = np.ascontiguousarray(a)
        t[name] = nc.dram_tensor(f"in_{name}", a.shape, mybir.dt.from_np(a.dtype), kind="ExternalInput").ap()
    for name in ("k_parts", "q_parts"):
        t[name] = nc.dram_tensor(name, (B, 3, ND, P, S), BF16, kind="Internal").ap()
    t["out"] = nc.dram_tensor("out_0", (B, S, D), F32, kind="ExternalOutput").ap()
    build(nc, t)
    r = run_bass_kernel_spmd(nc, [arrays], core_ids=[0])
    return r.results[0]["out_0"]
```
